# Optimizing a Trainium2 kernel written in Bass

```python
import numpy as np
import jax
import jax.numpy as jnp

def _softmax(x, axis=-1):
    return jax.nn.softmax(x, axis=axis)

def _gelu(x):
    return jax.nn.gelu(x, approximate=True)

def _silu(x):
    return jax.nn.silu(x)

def _sigmoid(x):
    return jax.nn.sigmoid(x)

def _layernorm(x, axis=-1, eps=1e-05):
    m = jnp.mean(x, axis=axis, keepdims=True)
    v = jnp.var(x, axis=axis, keepdims=True)
    return (x - m) / jnp.sqrt(v + eps)

def _scatter_add(tgt, idx, src, axis=0):
    return tgt.at[idx].add(src)

def _segment_sum(src, seg, n):
    return jax.ops.segment_sum(src, seg, n)
kernel_name = 'mk_early_fusion_d1_tok_img4096_r4_d1d05e'

def setup_inputs(seed: int=0):
    np.random.seed(seed)
    _w = jnp.asarray

    def _rec_inputs():
        import jax
        import jax.numpy as jnp
        _rk = jax.random.key(seed)
        x = -0.00348982 + 0.707501 * jax.random.normal(jax.random.fold_in(_rk, 1), (16, 128, 64, 2), jnp.float32)
        txt = 6.73332e-06 + 0.02 * jax.random.normal(jax.random.fold_in(_rk, 2), (16, 32, 1024), jnp.float32)
        return (x, txt)
    x, txt = _rec_inputs()

    def _L0_tok_setup():
        import jax, jax.numpy as jnp
        import numpy as np
        H, N, S, CH, LEN = (128, 64, 128, 1, 1024)

        def _s4d_kernel(log_dt, C, B, inv_A_real, A_imag, L):
            dt = jnp.exp(log_dt)
            Cc = C[..., 0] + 1j * C[..., 1]
            Bc = B[..., 0] + 1j * B[..., 1]
            A = -jnp.exp(inv_A_real) + 1j * A_imag
            rep = H // A.shape[0]
            A = jnp.tile(A, (rep, 1))
            Bc = jnp.tile(Bc, (rep, 1))
            dtA = A * dt[:, None]
            Cc = Bc[None, :, :] * Cc
            Cc = Cc * (jnp.exp(dtA) - 1.0) / A
            ell = jnp.arange(L, dtype=jnp.float32)
            V = jnp.exp(dtA[:, :, None] * ell)
            K = 2.0 * jnp.einsum('chn,hnl->chl', Cc, V).real
            return K.astype(jnp.float32)
        key = jax.random.key(seed)
        k1, k2 = jax.random.split(key, 2)
        log_dt = jax.random.uniform(k1, (H,), minval=float(np.log(0.001)), maxval=float(np.log(0.1))).astype(jnp.float32)
        inv_A_real = jnp.full((S, N), float(np.log(0.5)), dtype=jnp.float32)
        A_imag = jnp.tile((np.pi * jnp.arange(N, dtype=jnp.float32))[None, :], (S, 1))
        B = jnp.stack([jnp.ones((S, N), jnp.float32), jnp.zeros((S, N), jnp.float32)], axis=-1)
        C = (jax.random.normal(k2, (CH, H, N, 2)) * 0.5 ** 0.5).astype(jnp.float32)
        return {'log_dt': log_dt, 'C': C, 'B': B, 'inv_A_real': inv_A_real, 'A_imag': A_imag, 'L': LEN}
    _L0_tok_all = _L0_tok_setup()
    _L0_tok_in = {k: v for k, v in _L0_tok_all.items() if k in ('log_dt', 'B', 'inv_A_real', 'A_imag')}
    del _L0_tok_all

    def _L0_attn_setup():
        import jax, jax.numpy as jnp
        import numpy as np
        BLOCK_H = 32
        BLOCK_W = 32
        N_FEAT = 1024
        K_FEAT = 1024
        key = jax.random.key(seed)
        k1, k2, k3 = jax.random.split(key, 3)
        data = jax.random.normal(k1, (4, 256, K_FEAT), dtype=jnp.float32)
        weight = jax.random.normal(k2, (N_FEAT, K_FEAT), dtype=jnp.float32) * 0.02
        nb, kb = (N_FEAT // BLOCK_H, K_FEAT // BLOCK_W)
        block_pattern = jax.random.randint(k3, (nb, kb), 0, 2, dtype=jnp.int32)
        mask = jnp.repeat(jnp.repeat(block_pattern, BLOCK_H, axis=0), BLOCK_W, axis=1)
        return {'data': data, 'weight': weight, 'mask': mask}
    _L0_attn_all = _L0_attn_setup()
    _L0_attn_in = {k: v for k, v in _L0_attn_all.items() if k in ('weight', 'mask')}
    del _L0_attn_all

    def _L0_ffn_setup():
        import jax, jax.numpy as jnp
        import numpy as np
        B, T, D_IN, D_OUT = (8, 512, 1024, 1024)
        N_LORAS, RANK = (16, 32)
        SCALING = 1.0
        key = jax.random.key(seed)
        ks = jax.random.split(key, 8)
        std = 1.0 / D_IN ** 0.5
        x = jax.random.normal(ks[0], (B, T, D_IN), dtype=jnp.float32)
        idx = jax.random.randint(ks[1], (B,), 0, N_LORAS)
        gate = jax.nn.one_hot(idx, N_LORAS, dtype=jnp.float32)
        kernel = jax.random.normal(ks[2], (D_IN, D_OUT), dtype=jnp.float32) * std
        bias = jnp.zeros((D_OUT,), dtype=jnp.float32)
        lora_A = jax.random.normal(ks[3], (N_LORAS, RANK, D_IN), dtype=jnp.float32) * std
        lora_B = jax.random.normal(ks[4], (N_LORAS, D_OUT, RANK), dtype=jnp.float32) * 0.01
        lora_A_shared = jax.random.normal(ks[5], (RANK, D_IN), dtype=jnp.float32) * std
        lora_B_shared = jax.random.normal(ks[6], (D_OUT, RANK), dtype=jnp.float32) * 0.01
        return {'x': x, 'gate': gate, 'kernel': kernel, 'bias': bias, 'lora_A': lora_A, 'lora_B': lora_B, 'lora_A_shared': lora_A_shared, 'lora_B_shared': lora_B_shared}
    _L0_ffn_all = _L0_ffn_setup()
    _L0_ffn_in = {k: v for k, v in _L0_ffn_all.items() if k in ('gate', 'kernel', 'bias', 'lora_A', 'lora_B', 'lora_A_shared', 'lora_B_shared')}
    del _L0_ffn_all
    return {'x': x, 'txt': txt, 'L0_tok_log_dt': _L0_tok_in['log_dt'], 'L0_tok_B': _L0_tok_in['B'], 'L0_tok_inv_A_real': _L0_tok_in['inv_A_real'], 'L0_tok_A_imag': _L0_tok_in['A_imag'], 'L0_attn_weight': _L0_attn_in['weight'], 'L0_attn_mask': _L0_attn_in['mask'], 'L0_ffn_gate': _L0_ffn_in['gate'], 'L0_ffn_kernel': _L0_ffn_in['kernel'], 'L0_ffn_bias': _L0_ffn_in['bias'], 'L0_ffn_lora_A': _L0_ffn_in['lora_A'], 'L0_ffn_lora_B': _L0_ffn_in['lora_B'], 'L0_ffn_lora_A_shared': _L0_ffn_in['lora_A_shared'], 'L0_ffn_lora_B_shared': _L0_ffn_in['lora_B_shared']}

def reference(x, txt, L0_tok_log_dt, L0_tok_B, L0_tok_inv_A_real, L0_tok_A_imag, L0_attn_weight, L0_attn_mask, L0_ffn_gate, L0_ffn_kernel, L0_ffn_bias, L0_ffn_lora_A, L0_ffn_lora_B, L0_ffn_lora_A_shared, L0_ffn_lora_B_shared):
    import jax
    import jax.numpy as jnp

    def _L0_tok_ref(log_dt, C, B, inv_A_real, A_imag, L):
        import jax, jax.numpy as jnp
        import numpy as np
        H, N, S, CH, LEN = (128, 64, 128, 1, 1024)

        def _s4d_kernel(log_dt, C, B, inv_A_real, A_imag, L):
            dt = jnp.exp(log_dt)
            Cc = C[..., 0] + 1j * C[..., 1]
            Bc = B[..., 0] + 1j * B[..., 1]
            A = -jnp.exp(inv_A_real) + 1j * A_imag
            rep = H // A.shape[0]
            A = jnp.tile(A, (rep, 1))
            Bc = jnp.tile(Bc, (rep, 1))
            dtA = A * dt[:, None]
            Cc = Bc[None, :, :] * Cc
            Cc = Cc * (jnp.exp(dtA) - 1.0) / A
            ell = jnp.arange(L, dtype=jnp.float32)
            V = jnp.exp(dtA[:, :, None] * ell)
            K = 2.0 * jnp.einsum('chn,hnl->chl', Cc, V).real
            return K.astype(jnp.float32)
        return _s4d_kernel(log_dt, C, B, inv_A_real, A_imag, L)

    def _L0_attn_ref(data, weight, mask):
        import jax, jax.numpy as jnp
        import numpy as np
        BLOCK_H = 32
        BLOCK_W = 32
        N_FEAT = 1024
        K_FEAT = 1024
        N, K = weight.shape
        nb, kb = (N // BLOCK_H, K // BLOCK_W)
        block_mask = mask.reshape(nb, BLOCK_H, kb, BLOCK_W).astype(jnp.float32).sum(axis=(1, 3)) > 0
        elem_mask = jnp.repeat(jnp.repeat(block_mask, BLOCK_H, axis=0), BLOCK_W, axis=1)
        w_masked = weight * elem_mask.astype(weight.dtype)
        out = jnp.einsum('bsk,nk->bsn', data, w_masked)
        return out

    def _L0_ffn_ref(x, gate, kernel, bias, lora_A, lora_B, lora_A_shared, lora_B_shared):
        import jax, jax.numpy as jnp
        import numpy as np
        B, T, D_IN, D_OUT = (8, 512, 1024, 1024)
        N_LORAS, RANK = (16, 32)
        SCALING = 1.0
        base_out = jnp.matmul(x, kernel) + bias
        b = gate.shape[0]
        x_flat = x.reshape(b, -1, x.shape[-1])
        A_eff = jnp.einsum('bn,nri->bri', gate, lora_A)
        B_eff = jnp.einsum('bn,nor->bor', gate, lora_B)
        Ax = jnp.einsum('bri,bti->btr', A_eff, x_flat)
        delta_flat = jnp.einsum('bor,btr->bto', B_eff, Ax)
        Ax_s = jnp.einsum('ri,bti->btr', lora_A_shared, x_flat)
        delta_flat = delta_flat + jnp.einsum('or,btr->bto', lora_B_shared, Ax_s)
        delta = delta_flat.reshape(x.shape[:-1] + (kernel.shape[-1],))
        return base_out + (SCALING * delta).astype(base_out.dtype)
    h = _L0_tok_ref(L0_tok_log_dt, x, L0_tok_B, L0_tok_inv_A_real, L0_tok_A_imag, 1024)
    h = jnp.concatenate([h, txt], axis=1)
    h = h + _L0_attn_ref(_layernorm(h, axis=-1), L0_attn_weight, L0_attn_mask)
    h = h + _L0_ffn_ref(_layernorm(h, axis=-1), L0_ffn_gate, L0_ffn_kernel, L0_ffn_bias, L0_ffn_lora_A, L0_ffn_lora_B, L0_ffn_lora_A_shared, L0_ffn_lora_B_shared)
    return h

_drawn_inputs = setup_inputs


def setup_inputs(seed=0):
    import zlib

    import numpy as np

    out = dict(_drawn_inputs(seed))
    spreads = {'L0_tok_inv_A_real': (-0.6931471824645996, 0.2), 'L0_ffn_bias': (0.0, 0.1)}
    factors = {}
    for name, (base, spread) in spreads.items():
        noise = np.random.default_rng([zlib.crc32(name.encode()), seed]).standard_normal(out[name].shape)
        drawn = base * np.exp(spread * noise) if base else spread * noise
        out[name] = jnp.asarray(drawn.astype(out[name].dtype))
    for name, factor in factors.items():
        out[name] = (out[name] * factor).astype(out[name].dtype)
    return out
```

```python
import math
from contextlib import ExitStack

import concourse.bass as bass
from concourse import mybir


def build_fusion_layer(
    nc: bass.Bass,
    x: bass.AP,
    txt: bass.AP,
    log_dt: bass.AP,
    B: bass.AP,
    inv_A_real: bass.AP,
    A_imag: bass.AP,
    attn_w: bass.AP,
    attn_mask: bass.AP,
    gate: bass.AP,
    ffn_w: bass.AP,
    bias: bass.AP,
    lora_A: bass.AP,
    lora_B: bass.AP,
    lora_A_shared: bass.AP,
    lora_B_shared: bass.AP,
    out: bass.AP,
):
    F32, F32R, I32 = mybir.dt.float32, mybir.dt.float32r, mybir.dt.int32
    ALU, ACT, AX = mybir.AluOpType, mybir.ActivationFunctionType, mybir.AxisListType

    P = 128
    CH, H, N, _ = x.shape
    _, TXT, D = txt.shape
    ROWS = H + TXT
    NB, NLORA = gate.shape
    RANK = lora_A.shape[1]
    KC = D // P
    HALF = D // 2
    GR = 32
    NT = CH * GR // P
    CPT = CH // NT
    HBLK = H // GR
    GROUPS = HBLK + 1
    STEP, NA = P, D // P
    NB0, NB1 = 8, 16
    HS = GR // NT
    NE = NB0 + NB1 + NA
    GP = P // RANK
    NG = NLORA // GP
    LR = 3 * RANK
    LK = LR + 1
    OPB = D // P
    EPS = 1e-5
    MAGIC = 1.5 * 2.0 ** 23
    TWO_PI = 6.283185
    PI_1, PI_2, PI_3 = 6.28125, 1.93500518798828125e-3, 3.0199157663e-7
    LN2_HI, LN2_LO = 0.693359375, -2.12194440e-4

    taps = nc.dram_tensor("taps", [H, CH, D], F32, kind="Internal").ap()
    mid = nc.dram_tensor("mid", [GROUPS, NT, P, D], F32, kind="Internal").ap()

    ctx = ExitStack()
    with ctx:
        def sem(name):
            return ctx.enter_context(nc.semaphore(name))

        KB = 1024
        base = 16512
        at = {"end": base}

        def place(name, shape, dt, offset):
            size = 4
            for n in shape[1:]:
                size *= n
            at["end"] = offset + size
            return nc.alloc_sbuf_tensor_at(name, shape, dt, offset=offset)

        def after(name, shape, dt):
            return place(name, shape, dt, (at["end"] + 31) // 32 * 32)

        W0 = base
        w1_hi = place("w1_hi", [P, KC, D], F32R, W0)
        w1_lo = after("w1_lo", [P, KC, D], F32R)
        b_hi = place("b_hi", [LK, NT, D], F32R, W0)
        b_lo = after("b_lo", [LK, NT, D], F32R)
        S0 = W0 + 64 * KB
        c_re = place("c_re", [P, H, CH], F32, S0)
        c_im = after("c_im", [P, H, CH], F32)
        modes = after("modes", [P, 6, H], F32)
        turn = after("turn", [P, GR, NE], F32)
        mag = after("mag", [P, GR, NE], F32)
        decay = after("decay", [P, GR, NE], F32)
        SN = 2 * NB0 + 2 * NB1 + 3 * NA
        wave = after("wave", [P, GR, SN], F32)
        fdec = after("fdec", [P, 2, GR, NA], F32)
        lead = after("lead", [P, 2, GR, NA], F32)
        lead2 = after("lead2", [P, 2, GR, NA], F32)
        SR = at["end"]
        right = [after(f"right{i}", [P, HS, STEP], F32) for i in range(2)]
        left = [after(f"left{i}", [P, HS, CH, NA], F32) for i in range(2)]
        ST = at["end"]
        rtmp = after("rtmp", [P, HS, STEP], F32)
        ltmp = after("ltmp", [P, HS, CH, NA], F32)
        SK = at["end"]
        kst = [after(f"kst{i}", [P, HS, STEP], F32) for i in range(2)]
        assert at["end"] <= S0 + 80 * KB, at["end"] - S0
        x_nat = place("x_nat", [P, CH, N, 2], F32, ST)
        x_dup = place("x_dup", [P, 2, CH, 2, N], F32, S0 + 19 * KB)
        modes_in = place("modes_in", [P, 6, 2, N], F32, SR)
        XW = N + 1
        par = place("par", [P, 24, XW], F32, SK)
        pint = after("pint", [P, XW], I32)
        b_nat = after("b_nat", [P, N, 2], F32)
        a_nat = place("a_nat", [P, NG, D], F32, S0)
        bl_by_o = place("bl_by_o", [P, NG, OPB, GP, RANK], F32, S0)
        bl_nat = after("bl_nat", [P, NLORA, OPB, RANK], F32)
        b_tr = after("b_tr", [P, NG, D], F32)
        g_mat = after("g_mat", [P, NG, NB * RANK], F32)
        as_nat = after("as_nat", [RANK, D], F32)
        bs_nat = after("bs_nat", [P, OPB, RANK], F32)
        g_sel = after("g_sel", [NLORA, NG, P], F32)
        g_col = after("g_col", [P, NG, NB], F32)
        gate_t = after("gate_t", [NLORA, NB], F32)
        assert at["end"] <= S0 + 64 * KB
        w2_hi = place("w2_hi", [P, KC, D], F32R, S0)
        w2_lo = after("w2_lo", [P, KC, D], F32R)
        w2_raw = place("w2_raw", [P, KC, D], F32, S0 + 32 * KB)
        b_full = place("b_full", [LK, NT, D], F32, S0 + 64 * KB)
        A0 = S0 + 80 * KB
        w_nat = [place(f"w_nat{i}", [P, D], F32, A0 + i * 4 * KB) for i in range(2)]
        m_nat = [place(f"m_nat{i}", [P, D], I32, A0 + (8 + i * 4) * KB) for i in range(2)]
        a_hi = place("a_hi", [P, KC, NT, LR], F32R, A0)
        a_lo = after("a_lo", [P, KC, NT, LR], F32R)
        h_t = [place("h_t0", [P, D], F32, A0 + 24 * KB)] + [after(f"h_t{i}", [P, D], F32) for i in (1, 2, 3)]
        d_t = after("d_t", [P, D], F32)
        d_hi = [after(f"d_hi{i}", [P, KC, P], F32R) for i in range(2)]
        d_lo = [after(f"d_lo{i}", [P, KC, P], F32R) for i in range(2)]
        ident = after("ident", [P, P], F32)
        blocks = after("blocks", [P, P], F32)
        msum = [after(f"msum{i}", [P, D // 32], F32) for i in range(2)]
        etab = after("etab", [P, 2, NE], F32)
        half_pi = after("half_pi", [P, 2], F32)
        stat = after("stat", [P, 2, 6], F32)
        mv = after("mv", [P, 2], F32)
        sc = after("sc", [P, 8], F32)
        assert at["end"] <= 229368, at["end"]
        etab_i = place("etab_i", [P, 2, NE], I32, SK + 7 * KB + 512)
        rank_id = place("rank_id", [P, RANK], F32, S0 + 63 * KB)
        own_rows = place("own_rows", [LR, P], F32, W0 + 32 * KB)
        ax_f = after("ax_f", [LR, P], F32)
        ax_hi = [after(f"ax_hi{i}", [LK, P], F32R) for i in range(2)]
        ax_lo = [after(f"ax_lo{i}", [LK, P], F32R) for i in range(2)]

        def banks(name, n):
            return ctx.enter_context(nc.psum_tensor(name, [P, n * HALF], F32))

        acc = [banks(f"acc{i}", 2) for i in range(2)]
        tp = [banks(f"tp{i}", 1) for i in range(2)]
        side = [banks(f"side{i}", 1) for i in range(2)]

        dup_ok = [sem(f"dup_ok{i}") for i in range(2)]
        bl_ok = sem("bl_ok")
        const_ok = sem("const_ok")
        par_in = sem("par_in")
        x_in = sem("x_in")
        w_in = [sem(f"w_in{i}") for i in range(2)]
        h_in = [sem(f"h_in{i}") for i in range(4)]
        h_out = [sem(f"h_out{i}") for i in range(4)]
        own = sem("own")
        own_pool = sem("own_pool")
        etab_ok = sem("etab_ok")
        turn1_ok, sin1_ok = sem("turn1_ok"), sem("sin1_ok")
        modes_ok, msum_ok = sem("modes_ok"), sem("msum_ok")
        acc_free = sem("acc_free")
        tp_full = sem("tp_full")
        hi_ok = sem("hi_ok")
        lo_ok = sem("lo_ok")
        var_ok, sd_ok = sem("var_ok"), sem("sd_ok")
        d_ok = sem("d_ok")
        gemm_ok = sem("gemm_ok")
        tab_ok, wave_ok = sem("tab_ok"), sem("wave_ok")
        rmul_ok, r_ok, l_ok = sem("rmul_ok"), sem("r_ok"), sem("l_ok")
        k_ok, k_ev = sem("k_ok"), sem("k_ev")
        k_out = [sem(f"k_out{i}") for i in range(4)]
        gate_in = sem("gate_in")
        la_in, lb_in = sem("la_in"), sem("lb_in")
        sel_ok, col_ok, g_ok = sem("sel_ok"), sem("col_ok"), sem("g_ok")
        a_ps, a_hi_ok, a_lo_ok = sem("a_ps"), sem("a_hi_ok"), sem("a_lo_ok")
        bt_ps, bt_ev = sem("bt_ps"), sem("bt_ev")
        bm_ps, bm_ev = sem("bm_ps"), sem("bm_ev")
        w2_in, w2_hi_ok, w2_lo_ok = sem("w2_in"), sem("w2_hi_ok"), sem("w2_lo_ok")
        rows_ok = sem("rows_ok")
        b_hi_ok, b_lo_ok = sem("b_hi_ok"), sem("b_lo_ok")
        ax_ps, ax_f_ok, ax_hi_ok, ax_lo_ok = sem("ax_ps"), sem("ax_f_ok"), sem("ax_hi_ok"), sem("ax_lo_ok")

        WU = KC
        G1 = GROUPS * NT
        KU = 10

        def h_count(phase, m):
            if phase == 1:
                return 64 * m + 16
            return 64 * HBLK + 32 + 16 * m

        block = ctx.enter_context(nc.Block())

        @block.sync
        def _(sp):
            sp.dma_start(par[:, 0, 0:N], A_imag).then_inc(par_in, 16)
            sp.dma_start(par[:, 1, 0:N], inv_A_real).then_inc(par_in, 16)
            sp.dma_start(par[:, 1, N:XW], log_dt.rearrange("(h o) -> h o", o=1)).then_inc(par_in, 16)
            sp.dma_start(b_nat[:, :, :], B).then_inc(par_in, 16)

            def load_w(i, slot):
                sp.dma_start(m_nat[slot][:, :], attn_mask[bass.ds(i * P, P), :]).then_inc(w_in[slot], 16)
                sp.dma_start(w_nat[slot][:, :], attn_w[bass.ds(i * P, P), :]).then_inc(w_in[slot], 16)

            load_w(0, 0)
            sp.dma_start(x_nat[:, :, :, :], x.rearrange("c h n z -> h c n z")).then_inc(x_in, 16)
            load_w(1, 1)
            for s in range(NT):
                sp.dma_start(h_t[s][:, :], txt[CPT * s:CPT * (s + 1), :, :].rearrange("c t d -> (c t) d"))\
                  .then_inc(h_in[s], 16)
            with sp.Fori(1, KC // 2) as j:
                for slot in range(2):
                    sp.wait_ge(msum_ok, 2 * j + slot - 1)
                    sp.wait_ge(tp_full, 2 * (2 * j + slot) - 2)
                    load_w(2 * j + slot, slot)

            def store_taps(m, s):
                sp.wait_ge(k_ev, KU + 2 * (NT * m + s) + 2)
                sp.dma_start(taps[bass.ds(GR * m + HS * s, HS), :, :].rearrange("h c (a b) -> (c a) h b", b=STEP),
                             kst[s % 2][:, :, :]).then_inc(k_out[s], 16)

            def store_mid(m, s):
                sp.wait_ge(acc_free, WU + NT * m + s + 1)
                sp.dma_start(mid[bass.ds(m, 1), s, :, :].rearrange("o p d -> (o p) d"), h_t[s][:, :])\
                  .then_inc(h_out[s], 16)

            def load_block(m, s):
                sp.wait_ge(h_out[s], 16 * (m + 1))
                for c in range(CPT):
                    sp.dma_start(h_t[s][c * GR:(c + 1) * GR, :],
                                 taps[bass.ds(GR * m, GR), CPT * s + c, :]).then_inc(h_in[s], 16)

            def load_mid(g, slot, s):
                sp.dma_start(h_t[s][:, :], mid[bass.ds(slot, 1), s, :, :].rearrange("o p d -> (o p) d"))\
                  .then_inc(h_in[s], 16)

            def block_io(m, lora):
                for s in range(NT):
                    store_taps(m, s)
                    if s < NT - 1:
                        store_mid(m, s)
                for s in range(NT):
                    sp.wait_ge(k_out[s], 16 * (m + 1))
                for s in range(NT - 1):
                    load_block(m, s)
                if lora:
                    sp.dma_start(gate_t[:, :], gate.rearrange("b n -> n b"),
                                 allow_slow_non_contiguous=True).then_inc(gate_in, 16)
                    sp.dma_start(a_nat[:, :, :], lora_A.rearrange("(g n) r i -> (n r) g i", n=GP)).then_inc(la_in, 16)
                    sp.dma_start(as_nat[:, :], lora_A_shared).then_inc(la_in, 16)
                    sp.dma_start(bl_nat[:, :, :, :], lora_B.rearrange("n (p c) r -> p n c r", c=OPB)).then_inc(lb_in, 16)
                    sp.dma_start(bs_nat[:, :, :], lora_B_shared.rearrange("(p c) r -> p c r", c=OPB)).then_inc(lb_in, 16)
                    sp.dma_start(b_full[LR:LK, :, :], bias.rearrange("(o n) -> o n", o=1).unsqueeze(1)
                                 .to_broadcast([1, NT, D])).then_inc(lb_in, 16)
                store_mid(m, NT - 1)
                load_block(m, NT - 1)

            with sp.Fori(0, HBLK - 1) as m:
                block_io(m, False)
            block_io(HBLK - 1, True)

            last = HBLK
            store_mid(last, 0)
            sp.wait_ge(bm_ev, 4)
            sp.dma_start(w2_raw[:, :, :], ffn_w.rearrange("(k p) n -> p k n", p=P)).then_inc(w2_in, 16)
            for s in range(1, NT):
                store_mid(last, s)
                sp.wait_ge(h_out[s - 1], 16 * GROUPS)
                load_mid(0, 1, s - 1)
            sp.wait_ge(h_out[NT - 1], 16 * GROUPS)
            load_mid(0, 1, NT - 1)

            def store_out(g, s):
                sp.wait_ge(acc_free, WU + G1 + NT * g + s + 1)
                for c in range(CPT):
                    sp.dma_start(out[CPT * s + c, bass.ds(GR * g, GR), :], h_t[s][c * GR:(c + 1) * GR, :])\
                      .then_inc(h_out[s], 16)

            def next_in(g, slot, s):
                sp.wait_ge(h_out[s], 16 * GROUPS + 64 * (g + 1))
                load_mid(g + 1, slot, s)

            def group_io(g, slot):
                for s in range(NT):
                    store_out(g, s)
                    if s:
                        next_in(g, slot, s - 1)
                next_in(g, slot, NT - 1)

            with sp.Fori(0, HBLK - 1) as g:
                group_io(g, g + 2)
            group_io(HBLK - 1, 0)
            for s in range(NT):
                store_out(HBLK, s)
            for s in range(NT):
                sp.wait_ge(h_out[s], 16 * GROUPS + 64 * GROUPS)

        def double(copy, z, g):
            return copy(x_dup[:, z, 4 * g:4 * g + 4, :, :],
                        x_nat[:, 4 * g:4 * g + 4, :, z].unsqueeze(2).to_broadcast([P, 4, 2, N])).then_inc(dup_ok[z], 1)

        @block.gpsimd
        def _(pool):
            n_own = [0]

            def then(ins):
                n_own[0] += 1
                ins.then_inc(own_pool, 1)
                pool.wait_ge(own_pool, n_own[0])

            nc.gpsimd.memset(blocks[:, :], 0.0).then_inc(own_pool, 1)
            nc.gpsimd.memset(half_pi[:, 0:1], math.pi / 2)
            nc.gpsimd.memset(half_pi[:, 1:2], -math.pi / 2)
            n_own[0] += 1
            then(nc.gpsimd.memset(ident[:, :], 0.0))
            for q in range(P // 32):
                then(nc.gpsimd.memset(blocks[32 * q:32 * (q + 1), 32 * q:32 * (q + 1)], 1.0))
            parts = ((0, NB0, 1), (NB0, NB1, NB0), (NB0 + NB1, NA, STEP))
            for e0, n, l in parts:
                nc.gpsimd.iota(etab_i[:, 0, e0:e0 + n], [[1, n]], base=0, channel_multiplier=0)
                nc.gpsimd.iota(etab_i[:, 1, e0:e0 + n], [[l, n]], base=0, channel_multiplier=0)
            nc.gpsimd.affine_select(out=ident[:, :], in_=ident[:, :], compare_op=ALU.not_equal, fill=1.0,
                                    base=0, pattern=[[-1, P]], channel_multiplier=1).then_inc(const_ok, 1)

            pool.wait_ge(x_in, 16)
            for g in range(4):
                double(nc.gpsimd.tensor_copy, 0, g)

            def add_right(m, s):
                pool.wait_ge(rmul_ok, NT * m + s + 1)
                nc.gpsimd.tensor_tensor(right[s % 2][:, :, :], right[s % 2][:, :, :], rtmp[:, :, :], ALU.add)\
                  .then_inc(r_ok, 1)

            with pool.Fori(0, HBLK) as m:
                for s in range(NT):
                    add_right(m, s)

            pool.wait_ge(gate_in, 16)
            then(nc.gpsimd.memset(g_sel[:, :, :], 0.0))
            nc.gpsimd.affine_select(out=g_sel[:, :, :].rearrange("n g (j r) -> n g j r", r=RANK),
                                    in_=g_sel[:, :, :].rearrange("n g (j r) -> n g j r", r=RANK),
                                    compare_op=ALU.not_equal, fill=1.0, base=0,
                                    pattern=[[-GP, NG], [-1, GP], [0, RANK]], channel_multiplier=1)\
              .then_inc(sel_ok, 1)

            pool.wait_ge(lb_in, 48)
            pool.wait_ge(a_ps, KC)
            for g in range(NG):
                nc.gpsimd.tensor_copy(bl_by_o[:, g, :, :, :],
                                      bl_nat[:, GP * g:GP * (g + 1), :, :].rearrange("p n c r -> p c n r"))\
                  .then_inc(bl_ok, 1)

            pool.wait_ge(gemm_ok, WU + G1)
            then(nc.gpsimd.memset(own_rows[2 * RANK:LR, :], 1.0))
            then(nc.gpsimd.memset(own_rows[0:2 * RANK, :], 0.0))
            for i in range(2):
                then(nc.gpsimd.memset(ax_hi[i][LR:LK, :].bitcast(F32), 1.0))
                then(nc.gpsimd.memset(ax_lo[i][LR:LK, :].bitcast(F32), 0.0))
            then(nc.gpsimd.memset(own_rows[0:RANK, 0:P // 2], 1.0))
            nc.gpsimd.memset(own_rows[RANK:2 * RANK, P // 2:P], 1.0).then_inc(rows_ok, 1)

        @block.scalar
        def _(act):
            def hi_unit(u, dst, t=None):
                if t is not None:
                    act.wait_ge(gemm_ok, WU + t)
                for b in range(2):
                    act.wait_ge(tp_full, 2 * u + b + 1)
                    nc.scalar.activation(dst[:, 4 * b:4 * b + 4, :],
                                         tp[b][:, :].rearrange("p (k r) -> p k r", k=4), ACT.Copy)\
                      .then_inc(hi_ok, 1)

            def std(t):
                act.wait_ge(var_ok, t + 1)
                nc.scalar.activation(sc[:, 1:2], sc[:, 0:1], ACT.Sqrt).then_inc(sd_ok, 1)

            def waves(m):
                act.wait_ge(tab_ok, m + 1)
                nc.scalar.activation(decay[:, :, :], decay[:, :, :], ACT.Exp)
                re, im = slice(0, N), slice(N, P)

                def put(part, w0, n, e0, form):
                    src = mag if form.endswith("cos") else turn
                    scale = {"cos": -TWO_PI, "-cos": TWO_PI, "sin": TWO_PI, "-sin": -TWO_PI}[form]
                    bias_ap = {"cos": half_pi[part, 0:1], "-cos": half_pi[part, 1:2]}.get(form, 0.0)
                    return nc.scalar.activation(wave[part, :, w0:w0 + n], src[part, :, e0:e0 + n], ACT.Sin,
                                                bias=bias_ap, scale=scale)

                put(re, 0, NB0, 0, "cos")
                put(im, 0, NB0, 0, "sin")
                put(re, NB0, NB0, 0, "sin")
                put(im, NB0, NB0, 0, "cos")
                w0, e0 = 2 * NB0, NB0
                put(slice(0, P), w0, NB1, e0, "cos")
                put(re, w0 + NB1, NB1, e0, "-sin")
                put(im, w0 + NB1, NB1, e0, "sin")
                w0, e0 = 2 * NB0 + 2 * NB1, NB0 + NB1
                put(re, w0, NA, e0, "cos")
                put(im, w0, NA, e0, "-sin")
                put(re, w0 + NA, NA, e0, "-sin")
                put(im, w0 + NA, NA, e0, "-cos")
                put(re, w0 + 2 * NA, NA, e0, "-cos")
                put(im, w0 + 2 * NA, NA, e0, "sin").then_inc(wave_ok, 1)

            def taps_out(m, s):
                if s >= 2:
                    act.wait_ge(k_out[s - 2], 16 * (m + 1))
                for b in range(2):
                    act.wait_ge(k_ok, KU + 2 * (NT * m + s) + b + 1)
                    nc.scalar.activation(kst[s % 2][:, 4 * b:4 * b + 4, :],
                                         side[b][:, :].rearrange("p (h b) -> p h b", b=STEP), ACT.Copy)\
                      .then_inc(k_ev, 1)

            act.wait_ge(x_in, 16)
            for g in range(4):
                double(nc.scalar.copy, 1, g)
            for g in range(8):
                act.wait_ge(k_ok, g + 1)
                dst = (c_re, c_im)[g // 4]
                nc.scalar.activation(dst[:, :, 4 * (g % 4):4 * (g % 4) + 4],
                                     side[g % 2][:, :].rearrange("p (c h) -> p h c", c=4), ACT.Copy)\
                  .then_inc(k_ev, 1)
            act.wait_ge(turn1_ok, 1)
            nc.scalar.activation(par[:, 2, 0:N], par[:, 4, 0:N], ACT.Sin, scale=TWO_PI)
            nc.scalar.activation(par[:, 3, 0:N], par[:, 4, 0:N], ACT.Sin, scale=TWO_PI / 2).then_inc(sin1_ok, 1)
            for g in range(2):
                act.wait_ge(k_ok, 8 + g + 1)
                n = (4, 2)[g]
                nc.scalar.activation(modes[:, 4 * g:4 * g + n, :],
                                     side[g][:, 0:n * P].rearrange("p (j h) -> p j h", j=n), ACT.Copy)\
                  .then_inc(k_ev, 1)
            with act.Fori(0, KC) as i:
                for b in range(2):
                    act.wait_ge(tp_full, 2 * i + b + 1)
                    nc.scalar.activation(w1_hi[:, 4 * b:4 * b + 4, bass.ds(i * P, P)],
                                         tp[b][:, :].rearrange("p (k r) -> p k r", k=4), ACT.Copy)\
                      .then_inc(hi_ok, 1)
            std(0)
            hi_unit(WU, d_hi[0], 0)
            waves(0)

            def part1(m, s, more):
                t = NT * m + s
                taps_out(m, s)
                if s == NT - 1 and more:
                    waves(m + 1)
                std(t + 1)
                hi_unit(WU + t + 1, d_hi[(s + 1) % 2], t)

            with act.Fori(0, HBLK - 1) as m:
                for s in range(NT):
                    part1(m, s, True)
            for s in range(NT):
                part1(HBLK - 1, s, False)

            t0 = NT * HBLK
            std(t0 + 1)
            hi_unit(WU + t0 + 1, d_hi[1], t0)
            for k in range(KC):
                act.wait_ge(a_ps, k + 1)
                nc.scalar.activation(a_hi[:, k, :, 0:2 * RANK],
                                     side[k % 2][:, 0:NB * RANK].rearrange("p (s r) -> p s r", s=NT), ACT.Copy)
                nc.scalar.activation(a_hi[:, k, :, 2 * RANK:LR],
                                     side[k % 2][:, NB * RANK:(NB + 1) * RANK].unsqueeze(1)
                                     .to_broadcast([P, NT, RANK]), ACT.Copy).then_inc(a_hi_ok, 1)
            for g in range(NG):
                for b in range(2):
                    act.wait_ge(bt_ps, 2 * g + b + 1)
                    nc.scalar.activation(b_tr[:, g, :].rearrange("q (o c) -> q c o", c=OPB)[:, 4 * b:4 * b + 4, :],
                                         side[b][:, :].rearrange("q (c o) -> q c o", c=4), ACT.Copy)\
                      .then_inc(bt_ev, 1)
            for b in range(2):
                act.wait_ge(bt_ps, 2 * NG + b + 1)
                for s in range(NT):
                    ins = nc.scalar.activation(
                        b_full[2 * RANK:LR, s, :].rearrange("q (o c) -> q c o", c=OPB)[:, 4 * b:4 * b + 4, :],
                        side[b][0:RANK, :].rearrange("q (c o) -> q c o", c=4), ACT.Copy)
                ins.then_inc(bt_ev, 1)
            for j in range(4):
                half, quad = j // 2, j % 2
                act.wait_ge(bm_ps, j + 1)
                for o in range(2):
                    ins = nc.scalar.activation(b_full[0:2 * RANK, 2 * quad + o, half * HALF:(half + 1) * HALF],
                                               side[j % 2][64 * o:64 * o + 64, :], ACT.Copy)
                ins.then_inc(bm_ev, 1)
            for s in (2, 3):
                std(t0 + s)
                hi_unit(WU + t0 + s, d_hi[s % 2], t0 + s - 1)
                if s == 2:
                    act.wait_ge(w2_in, 16)
                for k in range((s - 2) * KC // 2, (s - 1) * KC // 2):
                    nc.scalar.activation(w2_hi[:, k, :], w2_raw[:, k, :], ACT.Copy).then_inc(w2_hi_ok, 1)

            std(G1)
            hi_unit(WU + G1, d_hi[0], G1 - 1)
            act.wait_ge(gemm_ok, WU + G1)
            for s in range(NT):
                nc.scalar.activation(b_hi[:, s, :], b_full[:, s, :], ACT.Copy).then_inc(b_hi_ok, 1)

            def part2(g, s, more):
                t = G1 + NT * g + s
                act.wait_ge(ax_f_ok, t - G1 + 1)
                nc.scalar.activation(ax_hi[s % 2][0:LR, :], ax_f[:, :], ACT.Copy).then_inc(ax_hi_ok, 1)
                if more:
                    std(t + 1)
                    hi_unit(WU + t + 1, d_hi[(s + 1) % 2], t)

            with act.Fori(0, HBLK) as g:
                for s in range(NT):
                    part2(g, s, True)
            for s in range(NT):
                part2(HBLK, s, s < NT - 1)

        @block.vector
        def _(dve):
            V = nc.vector
            count = {"n": 0, "base": 0}

            def then(ins):
                count["n"] += 1
                ins.then_inc(own, 1)
                dve.wait_ge(own, count["base"] + count["n"])

            def repeat(iterations, per_iteration, body):
                first, start = count["n"], count["base"]
                with dve.Fori(0, iterations) as i:
                    count["base"] = i * per_iteration + start
                    body(i)
                assert count["n"] - first == per_iteration, count["n"] - first
                count["base"], count["n"] = start, first + iterations * per_iteration

            dve.wait_ge(par_in, 64)
            A = lambda j: par[:, j, 0:N]
            W = lambda j: par[:, j, :]

            def exp_parts(src, w, k, r, p, two_k):
                then(V.tensor_scalar(k, src, 1.0 / math.log(2.0), MAGIC, ALU.mult, ALU.add))
                then(V.tensor_scalar(k, k, MAGIC, None, ALU.subtract))
                then(V.scalar_tensor_tensor(r, k, -LN2_HI, src, ALU.mult, ALU.add))
                then(V.scalar_tensor_tensor(r, k, -LN2_LO, r, ALU.mult, ALU.add))
                then(V.tensor_scalar(p, r, 1.0 / math.factorial(7), None, ALU.mult))
                for n in range(6, 0, -1):
                    then(V.scalar_tensor_tensor(p, p, 1.0 / math.factorial(n), r, ALU.add, ALU.mult))
                then(V.tensor_scalar(two_k, k, 127.0, 2.0 ** 23, ALU.add, ALU.mult))

            def wrap(dst, src, tmp):
                then(V.tensor_scalar(tmp, src, MAGIC, MAGIC, ALU.add, ALU.subtract))
                then(V.tensor_tensor(dst, src, tmp, ALU.subtract))

            two_k = pint[:, :].bitcast(F32)
            exp_parts(W(1), XW, W(5), W(6), W(7), pint[:, :])
            then(V.scalar_tensor_tensor(W(8), W(7), 1.0, two_k, ALU.add, ALU.mult))
            dt = par[:, 8, N:XW]
            then(V.tensor_scalar(A(9), A(8), dt, -1.0, ALU.mult, ALU.mult))
            then(V.tensor_scalar(A(10), A(0), dt, None, ALU.mult))
            then(V.tensor_scalar(A(5), A(10), 1.0 / (2 * math.pi), MAGIC, ALU.mult, ALU.add))
            then(V.tensor_scalar(A(5), A(5), MAGIC, None, ALU.subtract))
            for part in (PI_1, PI_2, PI_3):
                then(V.scalar_tensor_tensor(A(10), A(5), -part, A(10), ALU.mult, ALU.add))
            then(V.tensor_scalar(A(6), A(10), 1.0 / (2 * math.pi), None, ALU.mult))
            wrap(A(4), A(6), A(5))
            V.tensor_copy(modes_in[:, 0, 0, :], A(4)).then_inc(turn1_ok, 1)
            for j, mul in ((1, NB0), (2, STEP)):
                then(V.tensor_scalar(A(6), A(4), float(mul), None, ALU.mult))
                wrap(modes_in[:, j, 0, :], A(6), A(5))
            V.tensor_copy(modes_in[:, 3, 0, :], A(9))
            exp_parts(A(9), N, A(5), A(6), A(7), pint[:, 0:N])
            tk = pint[:, 0:N].bitcast(F32)
            then(V.tensor_tensor(A(11), A(7), tk, ALU.mult))
            then(V.scalar_tensor_tensor(A(11), tk, -1.0, A(11), ALU.add, ALU.add))
            dve.wait_ge(sin1_ok, 1)
            then(V.scalar_tensor_tensor(A(12), A(3), -2.0, A(3), ALU.mult, ALU.mult))
            then(V.scalar_tensor_tensor(A(12), A(11), 1.0, A(12), ALU.add, ALU.mult))
            then(V.tensor_tensor(A(12), A(12), A(11), ALU.add))
            then(V.scalar_tensor_tensor(A(13), A(11), 1.0, A(2), ALU.add, ALU.mult))
            then(V.tensor_tensor(A(14), A(8), A(8), ALU.mult))
            then(V.tensor_tensor(A(15), A(0), A(0), ALU.mult))
            then(V.tensor_tensor(A(14), A(14), A(15), ALU.add))
            then(V.reciprocal(A(14), A(14)))
            then(V.tensor_tensor(A(15), A(13), A(0), ALU.mult))
            then(V.tensor_tensor(A(16), A(12), A(8), ALU.mult))
            then(V.tensor_tensor(A(15), A(15), A(16), ALU.subtract))
            then(V.scalar_tensor_tensor(A(15), A(15), 2.0, A(14), ALU.mult, ALU.mult))
            then(V.tensor_tensor(A(16), A(13), A(8), ALU.mult))
            then(V.tensor_tensor(A(17), A(12), A(0), ALU.mult))
            then(V.tensor_tensor(A(16), A(16), A(17), ALU.add))
            then(V.scalar_tensor_tensor(A(16), A(16), -2.0, A(14), ALU.mult, ALU.mult))
            b_re, b_im = b_nat[:, :, 0], b_nat[:, :, 1]
            then(V.tensor_tensor(A(17), b_re, A(15), ALU.mult))
            then(V.tensor_tensor(A(18), b_im, A(16), ALU.mult))
            then(V.tensor_tensor(modes_in[:, 4, 0, :], A(17), A(18), ALU.subtract))
            then(V.tensor_tensor(A(17), b_re, A(16), ALU.mult))
            then(V.tensor_tensor(A(18), b_im, A(15), ALU.mult))
            then(V.tensor_tensor(modes_in[:, 5, 0, :], A(17), A(18), ALU.add))
            V.tensor_copy(modes_in[:, :, 1, :], modes_in[:, :, 0, :]).then_inc(modes_ok, 1)
            dve.wait_ge(const_ok, 1)
            then(V.tensor_copy(etab[:, :, :], etab_i[:, :, :]))

            def mask_sums(i, slot, use):
                dve.wait_ge(w_in[slot], 32 * use)
                V.tensor_reduce(msum[slot][:, :], m_nat[slot][:, :].rearrange("p (k j) -> p k j", j=32),
                                AX.X, ALU.add).then_inc(msum_ok, 1)

            def mask_weight(i, slot):
                dve.wait_ge(gemm_ok, i + 1)
                V.scalar_tensor_tensor(w_nat[slot][:, :].rearrange("p (k j) -> p k j", j=32),
                                       acc[slot][:, 0:D // 32].unsqueeze(2).to_broadcast([P, D // 32, 32]), 0.0,
                                       w_nat[slot][:, :].rearrange("p (k j) -> p k j", j=32),
                                       ALU.is_gt, ALU.mult).then_inc(acc_free, 1)

            def lo_unit(u, hi, lo):
                for b in range(2):
                    dve.wait_ge(hi_ok, 2 * u + b + 1)
                    V.tensor_tensor(lo[:, 4 * b:4 * b + 4, :], tp[b][:, :].rearrange("p (k r) -> p k r", k=4),
                                    hi[:, 4 * b:4 * b + 4, :].bitcast(F32), ALU.subtract).then_inc(lo_ok, 1)

            def w_cols(t, i):
                return t[:, :, bass.ds(i * P, P)]

            mask_sums(0, 0, 1)
            with dve.Fori(0, KC // 2 - 1) as j:
                mask_weight(2 * j, 0)
                mask_sums(2 * j + 1, 1, j + 1)
                lo_unit(2 * j, w_cols(w1_hi, 2 * j), w_cols(w1_lo, 2 * j))
                mask_weight(2 * j + 1, 1)
                mask_sums(2 * j + 2, 0, j + 2)
                lo_unit(2 * j + 1, w_cols(w1_hi, 2 * j + 1), w_cols(w1_lo, 2 * j + 1))
            mask_weight(KC - 2, 0)
            mask_sums(KC - 1, 1, KC // 2)
            lo_unit(KC - 2, w_cols(w1_hi, KC - 2), w_cols(w1_lo, KC - 2))
            mask_weight(KC - 1, 1)
            lo_unit(KC - 1, w_cols(w1_hi, KC - 1), w_cols(w1_lo, KC - 1))

            def normalise(t, slot, in_count):
                dve.wait_ge(h_in[slot], in_count)
                V.bn_stats(stat[:, 0, :], h_t[slot][:, 0:HALF])
                V.bn_stats(stat[:, 1, :], h_t[slot][:, HALF:D])
                dve.drain()
                then(V.bn_aggr(mv[:, :], stat[:, :, :].rearrange("p a b -> p (a b)")))
                V.tensor_scalar(sc[:, 0:1], mv[:, 1:2], EPS, None, ALU.add).then_inc(var_ok, 1)
                dve.wait_ge(sd_ok, t + 1)
                then(V.reciprocal(sc[:, 2:3], sc[:, 1:2]))
                then(V.scalar_tensor_tensor(sc[:, 3:4], sc[:, 2:3], sc[:, 2:3], sc[:, 0:1], ALU.mult, ALU.mult))
                then(V.tensor_scalar(sc[:, 3:4], sc[:, 3:4], -0.5, 1.5, ALU.mult, ALU.add))
                then(V.tensor_tensor(sc[:, 4:5], sc[:, 2:3], sc[:, 3:4], ALU.mult))
                dve.wait_ge(tp_full, 2 * (WU + t))
                V.tensor_scalar(d_t[:, :], h_t[slot][:, :], mv[:, 0:1], sc[:, 4:5], ALU.subtract, ALU.mult)\
                 .then_inc(d_ok, 1)

            def add_rows(t, s):
                dve.wait_ge(gemm_ok, WU + t + 1)
                V.tensor_tensor(h_t[s][:, :], acc[s % 2][:, :], h_t[s][:, :], ALU.add).then_inc(acc_free, 1)

            def over_e(ap, n):
                return ap.unsqueeze(2).to_broadcast([P, GR, n])

            def over_h(ap, n):
                return ap.unsqueeze(1).to_broadcast([P, GR, n])

            def tables(m):
                def mode(j):
                    return modes[:, j, bass.ds(GR * m, GR)]

                for j, e0, n in ((0, 0, NB0), (1, NB0, NB1), (2, NB0 + NB1, NA)):
                    ins = V.tensor_tensor(turn[:, :, e0:e0 + n], over_e(mode(j), n),
                                          over_h(etab[:, 0, e0:e0 + n], n), ALU.mult)
                then(ins)
                wrap(turn[:, :, :], turn[:, :, :], mag[:, :, :])
                V.tensor_scalar(mag[:, :, :].bitcast(I32), turn[:, :, :].bitcast(I32), 0x7FFFFFFF, None,
                                ALU.bitwise_and)
                V.tensor_tensor(decay[:, :, :], over_e(mode(3), NE), over_h(etab[:, 1, :], NE), ALU.mult)\
                 .then_inc(tab_ok, 1)
                dve.wait_ge(wave_ok, m + 1)
                w0, e0 = 0, 0
                for n in (NB0, NB1):
                    pair = wave[:, :, w0:w0 + 2 * n].rearrange("p h (z n) -> p h z n", z=2)
                    V.tensor_tensor(pair, pair, decay[:, :, e0:e0 + n].unsqueeze(2).to_broadcast([P, GR, 2, n]),
                                    ALU.mult)
                    w0, e0 = w0 + 2 * n, e0 + n
                then(V.tensor_tensor(fdec[:, :, :, :],
                                     modes[:, 4:6, bass.ds(GR * m, GR)].unsqueeze(3).to_broadcast([P, 2, GR, NA]),
                                     decay[:, :, e0:e0 + NA].unsqueeze(1).to_broadcast([P, 2, GR, NA]), ALU.mult))
                for z, dst in ((0, lead), (1, lead2)):
                    ins = V.tensor_tensor(dst[:, :, :, :],
                                          wave[:, :, w0 + z * NA:w0 + (z + 2) * NA]
                                          .rearrange("p h (z n) -> p z h n", z=2),
                                          fdec[:, z, :, :].unsqueeze(1).to_broadcast([P, 2, GR, NA]), ALU.mult)
                then(ins)
                then(V.tensor_tensor(lead[:, :, :, :], lead[:, :, :, :], lead2[:, :, :, :], ALU.add))

            def factors(m, s):
                q = NT * m + s
                hs = slice(HS * s, HS * (s + 1))
                first = isinstance(m, int) and q == 0
                if not (isinstance(m, int) and q < 2):
                    dve.wait_ge(k_ok, KU + 2 * q - 2)
                w1 = 2 * NB0
                r4 = right[s % 2][:, :, :].rearrange("p h (b a) -> p h b a", a=NB0)
                t4 = rtmp[:, :, :].rearrange("p h (b a) -> p h b a", a=NB0)

                def outer(dst, w, x0):
                    return V.tensor_tensor(dst, wave[:, hs, w:w + NB1].unsqueeze(3).to_broadcast([P, HS, NB1, NB0]),
                                           wave[:, hs, x0:x0 + NB0].unsqueeze(2).to_broadcast([P, HS, NB1, NB0]),
                                           ALU.mult)

                outer(r4, w1, 0)
                if not first:
                    dve.wait_ge(r_ok, q)
                    dve.wait_ge(l_ok, q)
                outer(t4, w1 + NB1, NB0).then_inc(rmul_ok, 1)
                for z, (c_z, dst) in enumerate(((c_re, left[s % 2]), (c_im, ltmp))):
                    ins = V.tensor_tensor(dst[:, :, :, :],
                                          c_z[:, bass.ds(GR * m + HS * s, HS), :].unsqueeze(3)
                                          .to_broadcast([P, HS, CH, NA]),
                                          lead[:, z, hs, :].unsqueeze(2).to_broadcast([P, HS, CH, NA]), ALU.mult)
                then(ins)
                V.tensor_tensor(left[s % 2][:, :, :, :], left[s % 2][:, :, :, :], ltmp[:, :, :, :], ALU.add)\
                 .then_inc(l_ok, 1)

            normalise(0, 0, h_count(1, 0))
            dve.wait_ge(k_ev, KU)
            lo_unit(WU, d_hi[0], d_lo[0])
            tables(0)
            factors(0, 0)

            def part1(m, s, more):
                t = NT * m + s
                if s < NT - 1:
                    factors(m, s + 1)
                elif more:
                    tables(m + 1)
                    factors(m + 1, 0)
                normalise(t + 1, (s + 1) % NT, h_count(1, m + (s + 1) // NT))
                lo_unit(WU + t + 1, d_hi[(s + 1) % 2], d_lo[(s + 1) % 2])
                add_rows(t, s)

            OWN_PART1 = 30
            repeat(HBLK - 1, OWN_PART1, lambda m: [part1(m, s, True) for s in range(NT)])
            for s in range(NT):
                part1(HBLK - 1, s, False)

            t0 = NT * HBLK
            then(V.tensor_reduce(rank_id[:, :], ident[:, :].rearrange("p (j r) -> p r j", r=RANK), AX.X, ALU.add))
            dve.wait_ge(col_ok, 1)
            then(V.tensor_copy(g_col[:, :, :], side[0][:, 0:NG * NB].rearrange("p (g b) -> p g b", g=NG)))
            V.tensor_tensor(g_mat[:, :, :].rearrange("p g (b r) -> p (g b) r", r=RANK),
                            g_col[:, :, :].rearrange("p g b -> p (g b)").unsqueeze(2)
                            .to_broadcast([P, NG * NB, RANK]),
                            rank_id[:, :].unsqueeze(1).to_broadcast([P, NG * NB, RANK]), ALU.mult)\
             .then_inc(g_ok, 1)
            normalise(t0 + 1, 1, h_count(1, HBLK))
            lo_unit(WU + t0 + 1, d_hi[1], d_lo[1])
            add_rows(t0, 0)
            for k in range(KC):
                dve.wait_ge(a_hi_ok, k + 1)
                V.tensor_tensor(a_lo[:, k, :, 0:2 * RANK],
                                side[k % 2][:, 0:NB * RANK].rearrange("p (s r) -> p s r", s=NT),
                                a_hi[:, k, :, 0:2 * RANK].bitcast(F32), ALU.subtract)
                V.tensor_tensor(a_lo[:, k, :, 2 * RANK:LR],
                                side[k % 2][:, NB * RANK:(NB + 1) * RANK].unsqueeze(1).to_broadcast([P, NT, RANK]),
                                a_hi[:, k, :, 2 * RANK:LR].bitcast(F32), ALU.subtract).then_inc(a_lo_ok, 1)
            for s in (2, 3):
                normalise(t0 + s, s, h_count(1, HBLK))
                lo_unit(WU + t0 + s, d_hi[s % 2], d_lo[s % 2])
                add_rows(t0 + s - 1, s - 1)
                for k in range((s - 2) * KC // 2, (s - 1) * KC // 2):
                    dve.wait_ge(w2_hi_ok, k + 1)
                    V.tensor_tensor(w2_lo[:, k, :], w2_raw[:, k, :], w2_hi[:, k, :].bitcast(F32), ALU.subtract)\
                     .then_inc(w2_lo_ok, 1)
            add_rows(t0 + 3, 3)

            normalise(G1, 0, h_count(2, 0))
            lo_unit(WU + G1, d_hi[0], d_lo[0])
            for s in range(NT):
                dve.wait_ge(b_hi_ok, s + 1)
                V.tensor_tensor(b_lo[:, s, :], b_full[:, s, :], b_hi[:, s, :].bitcast(F32), ALU.subtract)\
                 .then_inc(b_lo_ok, 1)
            dve.wait_ge(rows_ok, 1)

            def part2(g, s, more):
                t = G1 + NT * g + s
                dve.wait_ge(ax_ps, t - G1 + 1)
                V.tensor_tensor(ax_f[:, :], side[s % 2][0:LR, 0:P], own_rows[:, :], ALU.mult).then_inc(ax_f_ok, 1)
                dve.wait_ge(ax_hi_ok, t - G1 + 1)
                V.tensor_tensor(ax_lo[s % 2][0:LR, :], ax_f[:, :], ax_hi[s % 2][0:LR, :].bitcast(F32), ALU.subtract)\
                 .then_inc(ax_lo_ok, 1)
                if more:
                    normalise(t + 1, (s + 1) % NT, h_count(2, g + (s + 1) // NT))
                    lo_unit(WU + t + 1, d_hi[(s + 1) % 2], d_lo[(s + 1) % 2])
                add_rows(t, s)

            OWN_PART2 = 20
            repeat(HBLK, OWN_PART2, lambda g: [part2(g, s, True) for s in range(NT)])
            for s in range(NT):
                part2(HBLK, s, s < NT - 1)

        @block.tensor
        def _(pe):
            mm = nc.tensor.matmul
            pe.wait_ge(const_ok, 1)
            for g in range(8):
                pe.wait_ge(dup_ok[g // 4], g % 4 + 1)
                if g >= 2:
                    pe.wait_ge(k_ev, g - 1)
                for j in range(4):
                    c, z = 4 * (g % 4) + j, g // 4
                    ins = nc.tensor.transpose(side[g % 2][:, j * P:(j + 1) * P],
                                              x_dup[:, z, c, :, :].rearrange("h t n -> h (t n)"), ident[:, :])
                ins.then_inc(k_ok, 1)
            pe.wait_ge(k_ev, 8)
            pe.wait_ge(modes_ok, 1)
            for g, n in ((0, 4), (1, 2)):
                for j in range(n):
                    ins = nc.tensor.transpose(side[g][:, j * P:(j + 1) * P],
                                              modes_in[:, 4 * g + j, :, :].rearrange("h z n -> h (z n)"), ident[:, :])
                ins.then_inc(k_ok, 1)

            def block_sums(i, slot):
                pe.wait_ge(msum_ok, i + 1)
                mm(acc[slot][:, 0:D // 32], blocks[:, :], msum[slot][:, :], start=True, stop=True)\
                  .then_inc(gemm_ok, 1)

            def transposes(u, src, first=False):
                for b in range(2):
                    if not first:
                        pe.wait_ge(lo_ok, 2 * u - 1 + b)
                    for j in range(4):
                        k = 4 * b + j
                        ins = nc.tensor.transpose(tp[b][:, j * P:(j + 1) * P], src[:, k * P:(k + 1) * P], ident[:, :])
                    ins.then_inc(tp_full, 1)

            def weight_tile(i, slot, first=False, last=False):
                pe.wait_ge(acc_free, i + 1)
                transposes(i, w_nat[slot], first)
                if not last:
                    block_sums(i + 1, 1 - slot)

            block_sums(0, 0)
            weight_tile(0, 0, first=True)
            weight_tile(1, 1)
            with pe.Fori(1, KC // 2 - 1) as j:
                for slot in range(2):
                    weight_tile(2 * j + slot, slot)
            weight_tile(KC - 2, 0)
            weight_tile(KC - 1, 1, last=True)

            def split_mm(dst, l_hi, l_lo, r_hi, r_lo, start, stop):
                mm(dst, l_hi, r_hi, start=start, stop=False)
                mm(dst, l_hi, r_lo, start=False, stop=False)
                return mm(dst, l_lo, r_hi, start=False, stop=stop)

            def tile_transposes(t):
                pe.wait_ge(d_ok, t + 1)
                transposes(WU + t, d_t)

            def product(s, chunks, r_hi, r_lo, end):
                for k in chunks:
                    for half in range(2):
                        cols = slice(half * HALF, (half + 1) * HALF)
                        ins = split_mm(acc[s % 2][:, cols], d_hi[s % 2][:, k, :], d_lo[s % 2][:, k, :],
                                       r_hi[:, k, cols], r_lo[:, k, cols], k == 0, end and k == KC - 1)
                return ins

            def begin(t):
                pe.wait_ge(lo_ok, 2 * (WU + t) + 2)
                pe.wait_ge(acc_free, WU + t - 1)

            def tile1(t, s, more=True):
                begin(t)
                product(s, range(0, KC // 2), w1_hi, w1_lo, True)
                if more:
                    tile_transposes(t + 1)
                product(s, range(KC // 2, KC), w1_hi, w1_lo, True).then_inc(gemm_ok, 1)

            def tap_products(m, s):
                q = NT * m + s
                pe.wait_ge(r_ok, q + 1)
                pe.wait_ge(l_ok, q + 1)
                pe.wait_ge(k_ev, KU + 2 * q)
                for h in range(HS):
                    ins = mm(side[h // 4][:, (h % 4) * STEP:(h % 4 + 1) * STEP],
                             left[s % 2][:, h, :, :].rearrange("p c a -> p (c a)"), right[s % 2][:, h, :],
                             start=True, stop=True)
                    if h % 4 == 3:
                        ins.then_inc(k_ok, 1)

            tile_transposes(0)
            with pe.Fori(0, HBLK) as m:
                for s in range(NT):
                    tap_products(m, s)
                    tile1(NT * m + s, s)

            t0 = NT * HBLK
            pe.wait_ge(sel_ok, 1)
            pe.wait_ge(k_ev, KU + 2 * t0)
            for g in range(NG):
                ins = mm(side[0][:, g * NB:(g + 1) * NB], g_sel[:, g, :], gate_t[:, :], start=True, stop=True)
            ins.then_inc(col_ok, 1)
            tile1(t0, 0)
            pe.wait_ge(g_ok, 1)
            pe.wait_ge(la_in, 32)
            for k in range(KC):
                if k >= 2:
                    pe.wait_ge(a_lo_ok, k - 1)
                cols = slice(k * P, (k + 1) * P)
                for g in range(NG):
                    mm(side[k % 2][:, 0:NB * RANK], a_nat[:, g, cols], g_mat[:, g, :], start=(g == 0), stop=(g == NG - 1))
                nc.tensor.transpose(side[k % 2][:, NB * RANK:(NB + 1) * RANK], as_nat[:, cols], ident[0:RANK, 0:RANK])\
                  .then_inc(a_ps, 1)
            pe.wait_ge(a_lo_ok, KC)
            pe.wait_ge(lb_in, 48)
            for g in range(NG + 1):
                if g < NG:
                    pe.wait_ge(bl_ok, g + 1)
                for b in range(2):
                    n = 2 * g + b
                    if n >= 2:
                        pe.wait_ge(bt_ev, n - 1)
                    for j in range(4):
                        c = 4 * b + j
                        if g < NG:
                            ins = nc.tensor.transpose(side[b][:, j * P:(j + 1) * P],
                                                      bl_by_o[:, g, c, :, :].rearrange("p n r -> p (n r)"), ident[:, :])
                        else:
                            ins = nc.tensor.transpose(side[b][0:RANK, j * P:(j + 1) * P], bs_nat[:, c, :], ident[:, :])
                    ins.then_inc(bt_ps, 1)
            pe.wait_ge(bt_ev, 2 * NG + 2)
            for j in range(4):
                half, quad = j // 2, j % 2
                if j >= 2:
                    pe.wait_ge(bm_ev, j - 1)
                for g in range(NG):
                    ins = mm(side[j % 2][:, :], g_mat[:, g, quad * P:(quad + 1) * P],
                             b_tr[:, g, half * HALF:(half + 1) * HALF], start=(g == 0), stop=(g == NG - 1))
                ins.then_inc(bm_ps, 1)
            for s in range(1, NT):
                tile1(t0 + s, s, more=s < NT - 1)

            tile_transposes(G1)
            pe.wait_ge(bm_ev, 4)
            pe.wait_ge(w2_lo_ok, KC)

            def down(t, s):
                for k in range(KC):
                    ins = split_mm(side[s % 2][0:LR, 0:P], a_hi[:, k, s, :], a_lo[:, k, s, :],
                                   d_hi[s % 2][:, k, :], d_lo[s % 2][:, k, :], k == 0, k == KC - 1)
                ins.then_inc(ax_ps, 1)

            def up(t, s):
                pe.wait_ge(ax_lo_ok, t - G1 + 1)
                for half in range(2):
                    cols = slice(half * HALF, (half + 1) * HALF)
                    ins = split_mm(acc[s % 2][:, cols], ax_hi[s % 2][:, :], ax_lo[s % 2][:, :],
                                   b_hi[:, s, cols], b_lo[:, s, cols], False, True)
                return ins

            def tile2(g, s, more, first=False):
                t = G1 + NT * g + s
                begin(t)
                down(t, s)
                product(s, range(0, KC // 2), w2_hi, w2_lo, False)
                if more:
                    tile_transposes(t + 1)
                product(s, range(KC // 2, KC), w2_hi, w2_lo, False)
                if first:
                    pe.wait_ge(b_lo_ok, NT)
                up(t, s).then_inc(gemm_ok, 1)

            for s in range(NT):
                tile2(0, s, True, first=s == 0)
            with pe.Fori(1, HBLK) as g:
                for s in range(NT):
                    tile2(g, s, True)
            for s in range(NT):
                tile2(HBLK, s, s < NT - 1)


_INS = ['x', 'txt', 'L0_tok_log_dt', 'L0_tok_B', 'L0_tok_inv_A_real', 'L0_tok_A_imag', 'L0_attn_weight',
        'L0_attn_mask', 'L0_ffn_gate', 'L0_ffn_kernel', 'L0_ffn_bias', 'L0_ffn_lora_A', 'L0_ffn_lora_B',
        'L0_ffn_lora_A_shared', 'L0_ffn_lora_B_shared']
_OUTS = [((16, 160, 1024), 'float32')]


def kernel(**inputs):
    import numpy as _np
    import concourse.bacc as _bacc
    from concourse import mybir as _mybir
    from concourse.bass_utils import run_bass_kernel_spmd as _run

    nc = _bacc.Bacc("TRN2", target_bir_lowering=False, num_devices=1)
    arrays, args = {}, []
    for name in _INS:
        a = _np.ascontiguousarray(inputs[name])
        arrays[f"in_{name}_dram"] = a
        args.append(nc.dram_tensor(f"in_{name}_dram", a.shape, _mybir.dt.from_np(a.dtype), kind="ExternalInput").ap())
    for i, (shape, dtype) in enumerate(_OUTS):
        dt = _mybir.dt.from_np(_np.dtype(dtype))
        args.append(nc.dram_tensor(f"out_{i}_dram", shape, dt, kind="ExternalOutput").ap())
    build_fusion_layer(nc, *args)
    r = _run(nc, [arrays], core_ids=[0])
    got = tuple(r.results[0][f"out_{i}_dram"] for i in range(len(_OUTS)))
    return got[0]
```

```python
import math
from contextlib import ExitStack

import concourse.bass as bass
from concourse import mybir


def build_fusion_layer(
    nc: bass.Bass,
    x: bass.AP,
    txt: bass.AP,
    log_dt: bass.AP,
    B: bass.AP,
    inv_A_real: bass.AP,
    A_imag: bass.AP,
    attn_w: bass.AP,
    attn_mask: bass.AP,
    gate: bass.AP,
    ffn_w: bass.AP,
    bias: bass.AP,
    lora_A: bass.AP,
    lora_B: bass.AP,
    lora_A_shared: bass.AP,
    lora_B_shared: bass.AP,
    out: bass.AP,
):
    F32, F32R, I32 = mybir.dt.float32, mybir.dt.float32r, mybir.dt.int32
    ALU, ACT, AX = mybir.AluOpType, mybir.ActivationFunctionType, mybir.AxisListType

    P = 128
    CH, H, N, _ = x.shape
    _, TXT, D = txt.shape
    ROWS = H + TXT
    NB, NLORA = gate.shape
    RANK = lora_A.shape[1]
    KC = D // P
    HALF = D // 2
    GR = 32
    NT = CH * GR // P
    CPT = CH // NT
    HBLK = H // GR
    GROUPS = HBLK + 1
    STEP, NA = P, D // P
    NB0, NB1 = 8, 16
    HS = GR // NT
    NE = NB0 + NB1 + NA
    GP = P // RANK
    NG = NLORA // GP
    LR = 3 * RANK
    LK = LR + 1
    OPB = D // P
    EPS = 1e-5
    MAGIC = 1.5 * 2.0 ** 23
    TWO_PI = 6.283185
    PI_1, PI_2, PI_3 = 6.28125, 1.93500518798828125e-3, 3.0199157663e-7
    LN2_HI, LN2_LO = 0.693359375, -2.12194440e-4

    taps = nc.dram_tensor("taps", [H, CH, D], F32, kind="Internal").ap()
    mid = nc.dram_tensor("mid", [GROUPS, NT, P, D], F32, kind="Internal").ap()

    ctx = ExitStack()
    with ctx:
        def sem(name):
            return ctx.enter_context(nc.semaphore(name))

        KB = 1024
        base = 16512
        at = {"end": base}

        def place(name, shape, dt, offset):
            size = 4
            for n in shape[1:]:
                size *= n
            at["end"] = offset + size
            return nc.alloc_sbuf_tensor_at(name, shape, dt, offset=offset)

        def after(name, shape, dt):
            return place(name, shape, dt, (at["end"] + 31) // 32 * 32)

        W0 = base
        w1_hi = place("w1_hi", [P, KC, D], F32R, W0)
        w1_lo = after("w1_lo", [P, KC, D], F32R)
        b_hi = place("b_hi", [LK, NT, D], F32R, W0)
        b_lo = after("b_lo", [LK, NT, D], F32R)
        S0 = W0 + 64 * KB
        c_re = place("c_re", [P, H, CH], F32, S0)
        c_im = after("c_im", [P, H, CH], F32)
        modes = after("modes", [P, 6, H], F32)
        turn = after("turn", [P, GR, NE], F32)
        mag = after("mag", [P, GR, NE], F32)
        decay = after("decay", [P, GR, NE], F32)
        SN = 2 * NB0 + 2 * NB1 + 3 * NA
        wave = after("wave", [P, GR, SN], F32)
        fdec = after("fdec", [P, 2, GR, NA], F32)
        lead = after("lead", [P, 2, GR, NA], F32)
        lead2 = after("lead2", [P, 2, GR, NA], F32)
        SR = at["end"]
        right = [after(f"right{i}", [P, HS, STEP], F32) for i in range(2)]
        left = [after(f"left{i}", [P, HS, CH, NA], F32) for i in range(2)]
        ST = at["end"]
        rtmp = after("rtmp", [P, HS, STEP], F32)
        ltmp = after("ltmp", [P, HS, CH, NA], F32)
        SK = at["end"]
        kst = [after(f"kst{i}", [P, HS, STEP], F32) for i in range(2)]
        assert at["end"] <= S0 + 80 * KB, at["end"] - S0
        x_nat = place("x_nat", [P, CH, N, 2], F32, ST)
        x_dup = place("x_dup", [P, 2, CH, 2, N], F32, S0 + 19 * KB)
        modes_in = place("modes_in", [P, 6, 2, N], F32, SR)
        XW = N + 1
        par = place("par", [P, 24, XW], F32, SK)
        pint = after("pint", [P, XW], I32)
        b_nat = after("b_nat", [P, N, 2], F32)
        a_nat = place("a_nat", [P, NG, D], F32, S0)
        bl_by_o = place("bl_by_o", [P, NG, OPB, GP, RANK], F32, S0)
        bl_nat = after("bl_nat", [P, NLORA, OPB, RANK], F32)
        b_tr = after("b_tr", [P, NG, D], F32)
        g_mat = after("g_mat", [P, NG, NB * RANK], F32)
        as_nat = after("as_nat", [RANK, D], F32)
        bs_nat = after("bs_nat", [P, OPB, RANK], F32)
        g_sel = after("g_sel", [NLORA, NG, P], F32)
        g_col = after("g_col", [P, NG, NB], F32)
        gate_t = after("gate_t", [NLORA, NB], F32)
        assert at["end"] <= S0 + 64 * KB
        w2_hi = place("w2_hi", [P, KC, D], F32R, S0)
        w2_lo = after("w2_lo", [P, KC, D], F32R)
        w2_raw = place("w2_raw", [P, KC, D], F32, S0 + 32 * KB)
        b_full = place("b_full", [LK, NT, D], F32, S0 + 64 * KB)
        A0 = S0 + 80 * KB
        w_nat = [place(f"w_nat{i}", [P, D], F32, A0 + i * 4 * KB) for i in (0, 1, 2, 8)]
        m_nat = [place(f"m_nat{i}", [P, D], I32, A0 + i * 4 * KB) for i in (3, 4, 5, 9)]
        a_hi = place("a_hi", [P, KC, NT, LR], F32R, A0)
        a_lo = after("a_lo", [P, KC, NT, LR], F32R)
        h_t = [place("h_t0", [P, D], F32, A0 + 24 * KB)] + [after(f"h_t{i}", [P, D], F32) for i in (1, 2, 3)]
        d_t = after("d_t", [P, D], F32)
        d_hl = [after(f"d_hl{i}", [P, KC, 2, P], F32R) for i in range(2)]
        d_hi, d_lo = ([d[:, :, z, :] for d in d_hl] for z in range(2))
        ident = after("ident", [P, P], F32)
        blocks = after("blocks", [P, P], F32)
        msum = [after(f"msum{i}", [P, D // 32], F32) for i in range(2)]
        etab = after("etab", [P, 2, NE], F32)
        half_pi = after("half_pi", [P, 2], F32)
        stat = after("stat", [P, 2, 6], F32)
        mv = after("mv", [P, 2], F32)
        sc = after("sc", [P, 8], F32)
        assert at["end"] <= 229368, at["end"]
        etab_i = place("etab_i", [P, 2, NE], I32, SK + 7 * KB + 512)
        rank_id = place("rank_id", [P, RANK], F32, S0 + 63 * KB)
        own_rows = place("own_rows", [LR, P], F32, W0 + 32 * KB)
        ax_f = after("ax_f", [LR, P], F32)
        ax_g = after("ax_g", [LR, P], F32)
        ax_hi = [after(f"ax_hi{i}", [LK, P], F32R) for i in range(2)]
        ax_lo = [after(f"ax_lo{i}", [LK, P], F32R) for i in range(2)]

        def banks(name, n):
            return ctx.enter_context(nc.psum_tensor(name, [P, n * HALF], F32))

        acc = [banks(f"acc{i}", 2) for i in range(2)]
        tp = [banks(f"tp{i}", 1) for i in range(2)]
        side = [banks(f"side{i}", 1) for i in range(2)]

        dup_ok = [sem(f"dup_ok{i}") for i in range(2)]
        bl_ok = sem("bl_ok")
        const_ok = sem("const_ok")
        par_in = sem("par_in")
        x_in = sem("x_in")
        w_in = [sem(f"w_in{i}") for i in range(4)]
        h_in = [sem(f"h_in{i}") for i in range(4)]
        h_out = [sem(f"h_out{i}") for i in range(4)]
        own = sem("own")
        own_pool = sem("own_pool")
        den_ok, recip_ok = sem("den_ok"), sem("recip_ok")
        turn1_ok, sin1_ok = sem("turn1_ok"), sem("sin1_ok")
        modes_ok, msum_ok = sem("modes_ok"), sem("msum_ok")
        bs_ok, mask_ok = sem("bs_ok"), sem("mask_ok")
        acc_free = sem("acc_free")
        tp_full = sem("tp_full")
        hi_ok = sem("hi_ok")
        lo_ok = sem("lo_ok")
        var_ok, sd_ok = sem("var_ok"), sem("sd_ok")
        d_ok = sem("d_ok")
        gemm_ok = sem("gemm_ok")
        tab_ok, wave_ok = sem("tab_ok"), sem("wave_ok")
        rmul_ok, r_ok, l_ok = sem("rmul_ok"), sem("r_ok"), sem("l_ok")
        k_ok, k_ev = sem("k_ok"), sem("k_ev")
        k_out = [sem(f"k_out{i}") for i in range(4)]
        gate_in = sem("gate_in")
        la_in, lb_in = sem("la_in"), sem("lb_in")
        sel_ok, col_ok, g_ok = sem("sel_ok"), sem("col_ok"), sem("g_ok")
        a_ps, a_hi_ok, a_lo_ok = sem("a_ps"), sem("a_hi_ok"), sem("a_lo_ok")
        bt_ps, bt_ev = sem("bt_ps"), sem("bt_ev")
        bm_ps, bm_ev = sem("bm_ps"), sem("bm_ev")
        w2_in, w2_hi_ok, w2_lo_ok = sem("w2_in"), sem("w2_hi_ok"), sem("w2_lo_ok")
        rows_ok = sem("rows_ok")
        b_hi_ok, b_lo_ok = sem("b_hi_ok"), sem("b_lo_ok")
        ax_ps, ax_f_ok, ax_hi_ok, ax_lo_ok = sem("ax_ps"), sem("ax_f_ok"), sem("ax_hi_ok"), sem("ax_lo_ok")

        WU = KC
        EARLY = 2

        def tile_unit(t):
            return KC // 2 + t if isinstance(t, int) and t < EARLY else WU + t

        def weight_unit(i):
            return i if i < KC // 2 else i + EARLY

        G1 = GROUPS * NT
        KU = 10

        def h_count(phase, m):
            if phase == 1:
                return 64 * m + 16
            return 64 * HBLK + 32 + 16 * m

        block = ctx.enter_context(nc.Block())

        @block.sync
        def _(sp):
            def load_w(i):
                sp.dma_start(m_nat[i % 4][:, :], attn_mask[i * P:(i + 1) * P, :]).then_inc(w_in[i % 4], 16)
                sp.dma_start(w_nat[i % 4][:, :], attn_w[i * P:(i + 1) * P, :]).then_inc(w_in[i % 4], 16)

            def load_text(s):
                sp.dma_start(h_t[s][:, :], txt[CPT * s:CPT * (s + 1), :, :].rearrange("c t d -> (c t) d"))\
                  .then_inc(h_in[s], 16)

            load_w(0)
            sp.dma_start(par[:, 0, 0:N], A_imag).then_inc(par_in, 16)
            sp.dma_start(par[:, 1, 0:N], inv_A_real).then_inc(par_in, 16)
            sp.dma_start(par[:, 1, N:XW], log_dt.rearrange("(h o) -> h o", o=1)).then_inc(par_in, 16)
            sp.dma_start(b_nat[:, :, :], B).then_inc(par_in, 16)
            for i in range(1, 4):
                load_w(i)
            load_text(0)
            sp.dma_start(x_nat[:, :, :, :], x.rearrange("c h n z -> h c n z")).then_inc(x_in, 16)
            load_text(1)
            for i in range(4, KC):
                sp.wait_ge(msum_ok, i - 3)
                sp.wait_ge(tp_full, 2 * weight_unit(i - 4) + 2)
                load_w(i)
            sp.wait_ge(msum_ok, KC)
            sp.wait_ge(tp_full, 2 * weight_unit(KC - 1) + 2)
            load_text(2)
            load_text(3)

            def store_taps(m, s):
                sp.wait_ge(k_ev, KU + 2 * (NT * m + s) + 2)
                sp.dma_start(taps[bass.ds(GR * m + HS * s, HS), :, :].rearrange("h c (a b) -> (c a) h b", b=STEP),
                             kst[s % 2][:, :, :]).then_inc(k_out[s], 16)

            def store_mid(m, s):
                sp.wait_ge(acc_free, NT * m + s + 1)
                sp.dma_start(mid[bass.ds(m, 1), s, :, :].rearrange("o p d -> (o p) d"), h_t[s][:, :])\
                  .then_inc(h_out[s], 16)

            def load_block(m, s):
                sp.wait_ge(h_out[s], 16 * (m + 1))
                for c in range(CPT):
                    sp.dma_start(h_t[s][c * GR:(c + 1) * GR, :],
                                 taps[bass.ds(GR * m, GR), CPT * s + c, :]).then_inc(h_in[s], 16)

            def load_mid(g, slot, s):
                sp.dma_start(h_t[s][:, :], mid[bass.ds(slot, 1), s, :, :].rearrange("o p d -> (o p) d"))\
                  .then_inc(h_in[s], 16)

            def block_io(m, lora):
                first = isinstance(m, int) and m == 0
                if first:
                    store_mid(m, 0)
                store_taps(m, 0)
                if first:
                    store_mid(m, 1)
                store_taps(m, 1)
                if not first:
                    store_mid(m, 0)
                store_taps(m, 2)
                store_mid(m, 2 if first else 1)
                store_taps(m, 3)
                for s in range(NT):
                    sp.wait_ge(k_out[s], 16 * (m + 1))
                for s in range(NT - 2):
                    load_block(m, s)
                if lora:
                    sp.dma_start(gate_t[:, :], gate.rearrange("b n -> n b"),
                                 allow_slow_non_contiguous=True).then_inc(gate_in, 16)
                    sp.dma_start(a_nat[:, :, :], lora_A.rearrange("(g n) r i -> (n r) g i", n=GP)).then_inc(la_in, 16)
                    sp.dma_start(as_nat[:, :], lora_A_shared).then_inc(la_in, 16)
                    sp.dma_start(bl_nat[:, :, :, :], lora_B.rearrange("n (p c) r -> p n c r", c=OPB)).then_inc(lb_in, 16)
                    sp.dma_start(bs_nat[:, :, :], lora_B_shared.rearrange("(p c) r -> p c r", c=OPB)).then_inc(lb_in, 16)
                    sp.dma_start(b_full[LR:LK, :, :], bias.rearrange("(o n) -> o n", o=1).unsqueeze(1)
                                 .to_broadcast([1, NT, D])).then_inc(lb_in, 16)
                if not first:
                    store_mid(m, NT - 2)
                load_block(m, NT - 2)
                store_mid(m, NT - 1)
                load_block(m, NT - 1)

            block_io(0, False)
            with sp.Fori(1, HBLK - 1) as m:
                block_io(m, False)
            block_io(HBLK - 1, True)

            last = HBLK
            store_mid(last, 0)
            sp.wait_ge(bm_ev, 4)
            sp.dma_start(w2_raw[:, :, :], ffn_w.rearrange("(k p) n -> p k n", p=P)).then_inc(w2_in, 16)
            for s in range(1, NT):
                store_mid(last, s)
                sp.wait_ge(h_out[s - 1], 16 * GROUPS)
                load_mid(0, 1, s - 1)
            sp.wait_ge(h_out[NT - 1], 16 * GROUPS)
            load_mid(0, 1, NT - 1)

            def store_out(g, s):
                sp.wait_ge(acc_free, G1 + NT * g + s + 1)
                for c in range(CPT):
                    sp.dma_start(out[CPT * s + c, bass.ds(GR * g, GR), :], h_t[s][c * GR:(c + 1) * GR, :])\
                      .then_inc(h_out[s], 16)

            def next_in(g, slot, s):
                sp.wait_ge(h_out[s], 16 * GROUPS + 64 * (g + 1))
                load_mid(g + 1, slot, s)

            def group_io(g, slot):
                for s in range(NT):
                    store_out(g, s)
                    if s:
                        next_in(g, slot, s - 1)
                next_in(g, slot, NT - 1)

            with sp.Fori(0, HBLK - 1) as g:
                group_io(g, g + 2)
            group_io(HBLK - 1, 0)
            for s in range(NT):
                store_out(HBLK, s)
            for s in range(NT):
                sp.wait_ge(h_out[s], 16 * GROUPS + 64 * GROUPS)

        def double(copy, z, g):
            return copy(x_dup[:, z, 4 * g:4 * g + 4, :, :],
                        x_nat[:, 4 * g:4 * g + 4, :, z].unsqueeze(2).to_broadcast([P, 4, 2, N])).then_inc(dup_ok[z], 1)

        @block.gpsimd
        def _(pool):
            n_own = [0]

            def then(ins):
                n_own[0] += 1
                ins.then_inc(own_pool, 1)
                pool.wait_ge(own_pool, n_own[0])

            nc.gpsimd.memset(blocks[:, :], 0.0).then_inc(own_pool, 1)
            nc.gpsimd.memset(half_pi[:, 0:1], math.pi / 2)
            nc.gpsimd.memset(half_pi[:, 1:2], -math.pi / 2)
            n_own[0] += 1
            then(nc.gpsimd.memset(ident[:, :], 0.0))
            for q in range(P // 32):
                then(nc.gpsimd.memset(blocks[32 * q:32 * (q + 1), 32 * q:32 * (q + 1)], 1.0))
            parts = ((0, NB0, 1), (NB0, NB1, NB0), (NB0 + NB1, NA, STEP))
            for e0, n, l in parts:
                nc.gpsimd.iota(etab_i[:, 0, e0:e0 + n], [[1, n]], base=0, channel_multiplier=0)
                nc.gpsimd.iota(etab_i[:, 1, e0:e0 + n], [[l, n]], base=0, channel_multiplier=0)
            nc.gpsimd.affine_select(out=ident[:, :], in_=ident[:, :], compare_op=ALU.not_equal, fill=1.0,
                                    base=0, pattern=[[-1, P]], channel_multiplier=1).then_inc(const_ok, 1)

            G = nc.gpsimd
            pool.wait_ge(par_in, 64)
            A = lambda j: par[:, j, 0:N]
            W = lambda j: par[:, j, :]

            def fused(dst, a, scalar, b, op0, op1, w=N):
                then(G.tensor_scalar(par[:, 20, 0:w], a, scalar, None, op0))
                then(G.tensor_tensor(dst, par[:, 20, 0:w], b, op1))

            def exp_parts(src, w, k, r, p, two_k):
                then(G.tensor_scalar(k, src, 1.0 / math.log(2.0), MAGIC, ALU.mult, ALU.add))
                then(G.tensor_scalar(k, k, MAGIC, None, ALU.subtract))
                fused(r, k, -LN2_HI, src, ALU.mult, ALU.add, w)
                fused(r, k, -LN2_LO, r, ALU.mult, ALU.add, w)
                then(G.tensor_scalar(p, r, 1.0 / math.factorial(7), None, ALU.mult))
                for n in range(6, 0, -1):
                    fused(p, p, 1.0 / math.factorial(n), r, ALU.add, ALU.mult, w)
                then(G.tensor_scalar(two_k, k, 127.0, 2.0 ** 23, ALU.add, ALU.mult))

            def wrap(dst, src, tmp):
                then(G.tensor_scalar(tmp, src, MAGIC, MAGIC, ALU.add, ALU.subtract))
                then(G.tensor_tensor(dst, src, tmp, ALU.subtract))

            two_k = pint[:, :].bitcast(F32)
            exp_parts(W(1), XW, W(5), W(6), W(7), pint[:, :])
            fused(W(8), W(7), 1.0, two_k, ALU.add, ALU.mult, XW)
            dt = par[:, 8, N:XW]
            then(G.tensor_tensor(A(14), A(8), A(8), ALU.mult))
            then(G.tensor_tensor(A(15), A(0), A(0), ALU.mult))
            G.tensor_tensor(A(14), A(14), A(15), ALU.add).then_inc(den_ok, 1)
            then(G.tensor_scalar(A(9), A(8), dt, -1.0, ALU.mult, ALU.mult))
            then(G.tensor_scalar(A(10), A(0), dt, None, ALU.mult))
            then(G.tensor_scalar(A(5), A(10), 1.0 / (2 * math.pi), MAGIC, ALU.mult, ALU.add))
            then(G.tensor_scalar(A(5), A(5), MAGIC, None, ALU.subtract))
            for part in (PI_1, PI_2, PI_3):
                fused(A(10), A(5), -part, A(10), ALU.mult, ALU.add)
            then(G.tensor_scalar(A(6), A(10), 1.0 / (2 * math.pi), None, ALU.mult))
            wrap(A(4), A(6), A(5))
            G.tensor_copy(modes_in[:, 0, 0, :], A(4)).then_inc(turn1_ok, 1)
            for j, mul in ((1, NB0), (2, STEP)):
                then(G.tensor_scalar(A(6), A(4), float(mul), None, ALU.mult))
                wrap(modes_in[:, j, 0, :], A(6), A(5))
            G.tensor_copy(modes_in[:, 3, 0, :], A(9))
            exp_parts(A(9), N, A(5), A(6), A(7), pint[:, 0:N])
            tk = pint[:, 0:N].bitcast(F32)
            then(G.tensor_tensor(A(11), A(7), tk, ALU.mult))
            fused(A(11), tk, -1.0, A(11), ALU.add, ALU.add)
            pool.wait_ge(x_in, 16)
            for g in range(4):
                double(nc.gpsimd.tensor_copy, 0, g)
            pool.wait_ge(sin1_ok, 1)
            fused(A(12), A(3), -2.0, A(3), ALU.mult, ALU.mult)
            fused(A(12), A(11), 1.0, A(12), ALU.add, ALU.mult)
            then(G.tensor_tensor(A(12), A(12), A(11), ALU.add))
            fused(A(13), A(11), 1.0, A(2), ALU.add, ALU.mult)
            pool.wait_ge(recip_ok, 1)
            then(G.tensor_tensor(A(15), A(13), A(0), ALU.mult))
            then(G.tensor_tensor(A(16), A(12), A(8), ALU.mult))
            then(G.tensor_tensor(A(15), A(15), A(16), ALU.subtract))
            fused(A(15), A(15), 2.0, A(14), ALU.mult, ALU.mult)
            then(G.tensor_tensor(A(16), A(13), A(8), ALU.mult))
            then(G.tensor_tensor(A(17), A(12), A(0), ALU.mult))
            then(G.tensor_tensor(A(16), A(16), A(17), ALU.add))
            fused(A(16), A(16), -2.0, A(14), ALU.mult, ALU.mult)
            b_re, b_im = b_nat[:, :, 0], b_nat[:, :, 1]
            then(G.tensor_tensor(A(17), b_re, A(15), ALU.mult))
            then(G.tensor_tensor(A(18), b_im, A(16), ALU.mult))
            then(G.tensor_tensor(modes_in[:, 4, 0, :], A(17), A(18), ALU.subtract))
            then(G.tensor_tensor(A(17), b_re, A(16), ALU.mult))
            then(G.tensor_tensor(A(18), b_im, A(15), ALU.mult))
            then(G.tensor_tensor(modes_in[:, 5, 0, :], A(17), A(18), ALU.add))
            G.tensor_copy(modes_in[:, :, 1, :], modes_in[:, :, 0, :]).then_inc(modes_ok, 1)

            def add_right(m, s):
                pool.wait_ge(rmul_ok, NT * m + s + 1)
                nc.gpsimd.tensor_tensor(right[s % 2][:, :, :], right[s % 2][:, :, :], rtmp[:, :, :], ALU.add)\
                  .then_inc(r_ok, 1)

            with pool.Fori(0, HBLK) as m:
                for s in range(NT):
                    add_right(m, s)

            pool.wait_ge(gate_in, 16)
            then(nc.gpsimd.memset(g_sel[:, :, :], 0.0))
            nc.gpsimd.affine_select(out=g_sel[:, :, :].rearrange("n g (j r) -> n g j r", r=RANK),
                                    in_=g_sel[:, :, :].rearrange("n g (j r) -> n g j r", r=RANK),
                                    compare_op=ALU.not_equal, fill=1.0, base=0,
                                    pattern=[[-GP, NG], [-1, GP], [0, RANK]], channel_multiplier=1)\
              .then_inc(sel_ok, 1)

            pool.wait_ge(lb_in, 48)
            pool.wait_ge(a_ps, KC)
            for g in range(NG):
                nc.gpsimd.tensor_copy(bl_by_o[:, g, :, :, :],
                                      bl_nat[:, GP * g:GP * (g + 1), :, :].rearrange("p n c r -> p c n r"))\
                  .then_inc(bl_ok, 1)

            pool.wait_ge(gemm_ok, G1)
            then(nc.gpsimd.memset(own_rows[2 * RANK:LR, :], 1.0))
            then(nc.gpsimd.memset(own_rows[0:2 * RANK, :], 0.0))
            for i in range(2):
                then(nc.gpsimd.memset(ax_hi[i][LR:LK, :].bitcast(F32), 1.0))
                then(nc.gpsimd.memset(ax_lo[i][LR:LK, :].bitcast(F32), 0.0))
            then(nc.gpsimd.memset(own_rows[0:RANK, 0:P // 2], 1.0))
            nc.gpsimd.memset(own_rows[RANK:2 * RANK, P // 2:P], 1.0).then_inc(rows_ok, 1)

        @block.scalar
        def _(act):
            def hi_unit(u, dst):
                for b in range(2):
                    act.wait_ge(tp_full, 2 * u + b + 1)
                    nc.scalar.activation(dst[:, 4 * b:4 * b + 4, :],
                                         tp[b][:, :].rearrange("p (k r) -> p k r", k=4), ACT.Copy)\
                      .then_inc(hi_ok, 1)

            def hi_tile(t, s):
                if not (isinstance(t, int) and t < 2):
                    act.wait_ge(gemm_ok, t - 1)
                hi_unit(tile_unit(t), d_hi[s % 2])

            def std(t):
                act.wait_ge(var_ok, t + 1)
                nc.scalar.activation(sc[:, 1:2], sc[:, 0:1], ACT.Sqrt).then_inc(sd_ok, 1)

            def waves(m):
                act.wait_ge(tab_ok, m + 1)
                nc.scalar.activation(decay[:, :, :], decay[:, :, :], ACT.Exp)
                re, im = slice(0, N), slice(N, P)

                def put(part, w0, n, e0, form):
                    src = mag if form.endswith("cos") else turn
                    scale = {"cos": -TWO_PI, "-cos": TWO_PI, "sin": TWO_PI, "-sin": -TWO_PI}[form]
                    bias_ap = {"cos": half_pi[part, 0:1], "-cos": half_pi[part, 1:2]}.get(form, 0.0)
                    return nc.scalar.activation(wave[part, :, w0:w0 + n], src[part, :, e0:e0 + n], ACT.Sin,
                                                bias=bias_ap, scale=scale)

                put(re, 0, NB0, 0, "cos")
                put(im, 0, NB0, 0, "sin")
                put(re, NB0, NB0, 0, "sin")
                put(im, NB0, NB0, 0, "cos")
                w0, e0 = 2 * NB0, NB0
                put(slice(0, P), w0, NB1, e0, "cos")
                put(re, w0 + NB1, NB1, e0, "-sin")
                put(im, w0 + NB1, NB1, e0, "sin")
                w0, e0 = 2 * NB0 + 2 * NB1, NB0 + NB1
                put(re, w0, NA, e0, "cos")
                put(im, w0, NA, e0, "-sin")
                put(re, w0 + NA, NA, e0, "-sin")
                put(im, w0 + NA, NA, e0, "-cos")
                put(re, w0 + 2 * NA, NA, e0, "-cos")
                put(im, w0 + 2 * NA, NA, e0, "sin").then_inc(wave_ok, 1)

            def taps_out(m, s):
                if s >= 2:
                    act.wait_ge(k_out[s - 2], 16 * (m + 1))
                for b in range(2):
                    act.wait_ge(k_ok, KU + 2 * (NT * m + s) + b + 1)
                    nc.scalar.activation(kst[s % 2][:, 4 * b:4 * b + 4, :],
                                         side[b][:, :].rearrange("p (h b) -> p h b", b=STEP), ACT.Copy)\
                      .then_inc(k_ev, 1)

            def hi_weight(i):
                hi_unit(weight_unit(i), w1_hi[:, :, i * P:(i + 1) * P])

            def c_out(g):
                act.wait_ge(k_ok, g + 1)
                dst = (c_re, c_im)[g // 4]
                nc.scalar.activation(dst[:, :, 4 * (g % 4):4 * (g % 4) + 4],
                                     side[g % 2][:, :].rearrange("p (c h) -> p h c", c=4), ACT.Copy)\
                  .then_inc(k_ev, 1)

            for i in range(KC // 2):
                hi_weight(i)
            act.wait_ge(turn1_ok, 1)
            nc.scalar.activation(par[:, 2, 0:N], par[:, 4, 0:N], ACT.Sin, scale=TWO_PI)
            nc.scalar.activation(par[:, 3, 0:N], par[:, 4, 0:N], ACT.Sin, scale=TWO_PI / 2).then_inc(sin1_ok, 1)
            std(0)
            hi_tile(0, 0)
            act.wait_ge(x_in, 16)
            for g in range(4):
                double(nc.scalar.copy, 1, g)
            std(1)
            hi_tile(1, 1)
            for i in range(KC // 2, KC):
                c_out(2 * i - KC)
                c_out(2 * i - KC + 1)
                hi_weight(i)
            for g in range(2):
                act.wait_ge(k_ok, 8 + g + 1)
                n = (4, 2)[g]
                nc.scalar.activation(modes[:, 4 * g:4 * g + n, :],
                                     side[g][:, 0:n * P].rearrange("p (j h) -> p j h", j=n), ACT.Copy)\
                  .then_inc(k_ev, 1)
            waves(0)
            std(2)
            hi_tile(2, 2)
            taps_out(0, 0)
            std(3)
            taps_out(0, 1)
            hi_tile(3, 3)
            taps_out(0, 2)
            taps_out(0, 3)
            waves(1)
            std(4)
            hi_tile(4, 0)

            def part1(m, s, more):
                t = NT * m + s
                std(t + 1)
                if s == 0:
                    taps_out(m, 0)
                if s < NT - 1:
                    taps_out(m, s + 1)
                hi_tile(t + 1, s + 1)
                if s == 2 and more:
                    waves(m + 1)

            with act.Fori(1, HBLK - 1) as m:
                for s in range(NT):
                    part1(m, s, True)
            for s in range(NT):
                part1(HBLK - 1, s, False)

            t0 = NT * HBLK
            std(t0 + 1)
            hi_tile(t0 + 1, 1)
            for k in range(KC):
                act.wait_ge(a_ps, k + 1)
                nc.scalar.activation(a_hi[:, k, :, 0:2 * RANK],
                                     side[k % 2][:, 0:NB * RANK].rearrange("p (s r) -> p s r", s=NT), ACT.Copy)
                nc.scalar.activation(a_hi[:, k, :, 2 * RANK:LR],
                                     side[k % 2][:, NB * RANK:(NB + 1) * RANK].unsqueeze(1)
                                     .to_broadcast([P, NT, RANK]), ACT.Copy).then_inc(a_hi_ok, 1)
            for g in range(NG):
                for b in range(2):
                    act.wait_ge(bt_ps, 2 * g + b + 1)
                    nc.scalar.activation(b_tr[:, g, :].rearrange("q (o c) -> q c o", c=OPB)[:, 4 * b:4 * b + 4, :],
                                         side[b][:, :].rearrange("q (c o) -> q c o", c=4), ACT.Copy)\
                      .then_inc(bt_ev, 1)
            for b in range(2):
                act.wait_ge(bt_ps, 2 * NG + b + 1)
                for s in range(NT):
                    ins = nc.scalar.activation(
                        b_full[2 * RANK:LR, s, :].rearrange("q (o c) -> q c o", c=OPB)[:, 4 * b:4 * b + 4, :],
                        side[b][0:RANK, :].rearrange("q (c o) -> q c o", c=4), ACT.Copy)
                ins.then_inc(bt_ev, 1)
            for j in range(4):
                half, quad = j // 2, j % 2
                act.wait_ge(bm_ps, j + 1)
                for o in range(2):
                    ins = nc.scalar.activation(b_full[0:2 * RANK, 2 * quad + o, half * HALF:(half + 1) * HALF],
                                               side[j % 2][64 * o:64 * o + 64, :], ACT.Copy)
                ins.then_inc(bm_ev, 1)
            for s in (2, 3):
                std(t0 + s)
                hi_tile(t0 + s, s)
                if s == 2:
                    act.wait_ge(w2_in, 16)
                for k in range((s - 2) * KC // 2, (s - 1) * KC // 2):
                    nc.scalar.activation(w2_hi[:, k, :], w2_raw[:, k, :], ACT.Copy).then_inc(w2_hi_ok, 1)

            std(G1)
            hi_tile(G1, 0)
            act.wait_ge(gemm_ok, G1)
            for s in range(NT):
                nc.scalar.activation(b_hi[:, s, :], b_full[:, s, :], ACT.Copy).then_inc(b_hi_ok, 1)

            def part2(g, s, more):
                t = G1 + NT * g + s
                act.wait_ge(ax_f_ok, t - G1 + 1)
                nc.scalar.activation(ax_hi[s % 2][0:LR, :], ax_f[:, :], ACT.Copy).then_inc(ax_hi_ok, 1)
                if more:
                    std(t + 1)
                    hi_tile(t + 1, s + 1)

            with act.Fori(0, HBLK) as g:
                for s in range(NT):
                    part2(g, s, True)
            for s in range(NT):
                part2(HBLK, s, s < NT - 1)

        @block.vector
        def _(dve):
            V = nc.vector
            count = {"n": 0, "base": 0}

            def then(ins):
                count["n"] += 1
                ins.then_inc(own, 1)
                dve.wait_ge(own, count["base"] + count["n"])

            def repeat(begin, end, per_iteration, body):
                first, start = count["n"], count["base"]
                with dve.Fori(begin, end) as i:
                    count["base"] = i * per_iteration + (start - begin * per_iteration)
                    body(i)
                assert count["n"] - first == per_iteration, count["n"] - first
                count["base"], count["n"] = start, first + (end - begin) * per_iteration

            dve.wait_ge(const_ok, 1)
            then(V.tensor_copy(etab[:, :, :], etab_i[:, :, :]))

            def mask_sums(i):
                dve.wait_ge(w_in[i % 4], 32 * (i // 4 + 1))
                V.tensor_reduce(msum[i % 2][:, :], m_nat[i % 4][:, :].rearrange("p (k j) -> p k j", j=32),
                                AX.X, ALU.add).then_inc(msum_ok, 1)

            def mask_weight(i):
                dve.wait_ge(bs_ok, i + 1)
                rows = w_nat[i % 4][:, :].rearrange("p (k j) -> p k j", j=32)
                V.scalar_tensor_tensor(rows, acc[i % 2][:, HALF:HALF + D // 32].unsqueeze(2)
                                       .to_broadcast([P, D // 32, 32]), 0.0, rows,
                                       ALU.is_gt, ALU.mult).then_inc(mask_ok, 1)

            def lo_unit(u, hi, lo):
                for b in range(2):
                    dve.wait_ge(hi_ok, 2 * u + b + 1)
                    V.tensor_tensor(lo[:, 4 * b:4 * b + 4, :], tp[b][:, :].rearrange("p (k r) -> p k r", k=4),
                                    hi[:, 4 * b:4 * b + 4, :].bitcast(F32), ALU.subtract).then_inc(lo_ok, 1)

            def lo_weight(i):
                cols = slice(i * P, (i + 1) * P)
                lo_unit(weight_unit(i), w1_hi[:, :, cols], w1_lo[:, :, cols])

            def lo_tile(t, s):
                lo_unit(tile_unit(t), d_hi[s % 2], d_lo[s % 2])

            def normalise(t, slot, in_count):
                dve.wait_ge(h_in[slot], in_count)
                V.bn_stats(stat[:, 0, :], h_t[slot][:, 0:HALF])
                V.bn_stats(stat[:, 1, :], h_t[slot][:, HALF:D])
                dve.drain()
                then(V.bn_aggr(mv[:, :], stat[:, :, :].rearrange("p a b -> p (a b)")))
                V.tensor_scalar(sc[:, 0:1], mv[:, 1:2], EPS, None, ALU.add).then_inc(var_ok, 1)
                dve.wait_ge(sd_ok, t + 1)
                then(V.reciprocal(sc[:, 2:3], sc[:, 1:2]))
                then(V.scalar_tensor_tensor(sc[:, 3:4], sc[:, 2:3], sc[:, 2:3], sc[:, 0:1], ALU.mult, ALU.mult))
                then(V.tensor_scalar(sc[:, 3:4], sc[:, 3:4], -0.5, 1.5, ALU.mult, ALU.add))
                then(V.tensor_tensor(sc[:, 4:5], sc[:, 2:3], sc[:, 3:4], ALU.mult))
                if not (isinstance(t, int) and t == 0):
                    dve.wait_ge(tp_full, 2 * tile_unit(t - 1) + 2)
                V.tensor_scalar(d_t[:, :], h_t[slot][:, :], mv[:, 0:1], sc[:, 4:5], ALU.subtract, ALU.mult)\
                 .then_inc(d_ok, 1)

            def add_rows(t, s):
                dve.wait_ge(gemm_ok, t + 1)
                V.tensor_tensor(h_t[s][:, :], acc[s % 2][:, :], h_t[s][:, :], ALU.add).then_inc(acc_free, 1)

            def over_e(ap, n):
                return ap.unsqueeze(2).to_broadcast([P, GR, n])

            def over_h(ap, n):
                return ap.unsqueeze(1).to_broadcast([P, GR, n])

            def turns(m):
                def mode(j):
                    return modes[:, j, bass.ds(GR * m, GR)]

                for j, e0, n in ((0, 0, NB0), (1, NB0, NB1), (2, NB0 + NB1, NA)):
                    ins = V.tensor_tensor(turn[:, :, e0:e0 + n], over_e(mode(j), n),
                                          over_h(etab[:, 0, e0:e0 + n], n), ALU.mult)
                then(ins)
                then(V.tensor_scalar(mag[:, :, :], turn[:, :, :], MAGIC, MAGIC, ALU.add, ALU.subtract))
                then(V.tensor_tensor(turn[:, :, :], turn[:, :, :], mag[:, :, :], ALU.subtract))
                V.tensor_scalar(mag[:, :, :].bitcast(I32), turn[:, :, :].bitcast(I32), 0x7FFFFFFF, None,
                                ALU.bitwise_and)
                V.tensor_tensor(decay[:, :, :], over_e(mode(3), NE), over_h(etab[:, 1, :], NE), ALU.mult)\
                 .then_inc(tab_ok, 1)

            def tables(m):
                dve.wait_ge(wave_ok, m + 1)
                w0, e0 = 0, 0
                for n in (NB0, NB1):
                    pair = wave[:, :, w0:w0 + 2 * n].rearrange("p h (z n) -> p h z n", z=2)
                    V.tensor_tensor(pair, pair, decay[:, :, e0:e0 + n].unsqueeze(2).to_broadcast([P, GR, 2, n]),
                                    ALU.mult)
                    w0, e0 = w0 + 2 * n, e0 + n
                then(V.tensor_tensor(fdec[:, :, :, :],
                                     modes[:, 4:6, bass.ds(GR * m, GR)].unsqueeze(3).to_broadcast([P, 2, GR, NA]),
                                     decay[:, :, e0:e0 + NA].unsqueeze(1).to_broadcast([P, 2, GR, NA]), ALU.mult))
                for z, dst in ((0, lead), (1, lead2)):
                    ins = V.tensor_tensor(dst[:, :, :, :],
                                          wave[:, :, w0 + z * NA:w0 + (z + 2) * NA]
                                          .rearrange("p h (z n) -> p z h n", z=2),
                                          fdec[:, z, :, :].unsqueeze(1).to_broadcast([P, 2, GR, NA]), ALU.mult)
                then(ins)
                then(V.tensor_tensor(lead[:, :, :, :], lead[:, :, :, :], lead2[:, :, :, :], ALU.add))

            def factors(m, s):
                q = NT * m + s
                hs = slice(HS * s, HS * (s + 1))
                first = isinstance(m, int) and q == 0
                if not (isinstance(m, int) and q < 2):
                    dve.wait_ge(k_ok, KU + 2 * q - 2)
                w1 = 2 * NB0
                r4 = right[s % 2][:, :, :].rearrange("p h (b a) -> p h b a", a=NB0)
                t4 = rtmp[:, :, :].rearrange("p h (b a) -> p h b a", a=NB0)

                def outer(dst, w, x0):
                    return V.tensor_tensor(dst, wave[:, hs, w:w + NB1].unsqueeze(3).to_broadcast([P, HS, NB1, NB0]),
                                           wave[:, hs, x0:x0 + NB0].unsqueeze(2).to_broadcast([P, HS, NB1, NB0]),
                                           ALU.mult)

                outer(r4, w1, 0)
                if not first:
                    dve.wait_ge(r_ok, q)
                    dve.wait_ge(l_ok, q)
                outer(t4, w1 + NB1, NB0).then_inc(rmul_ok, 1)
                for z, (c_z, dst) in enumerate(((c_re, left[s % 2]), (c_im, ltmp))):
                    ins = V.tensor_tensor(dst[:, :, :, :],
                                          c_z[:, bass.ds(GR * m + HS * s, HS), :].unsqueeze(3)
                                          .to_broadcast([P, HS, CH, NA]),
                                          lead[:, z, hs, :].unsqueeze(2).to_broadcast([P, HS, CH, NA]), ALU.mult)
                then(ins)
                V.tensor_tensor(left[s % 2][:, :, :, :], left[s % 2][:, :, :, :], ltmp[:, :, :, :], ALU.add)\
                 .then_inc(l_ok, 1)

            def text(t):
                normalise(t, t, h_count(1, 0))

            mask_sums(0)
            mask_sums(1)
            mask_weight(0)
            mask_sums(2)
            mask_weight(1)
            mask_sums(3)
            lo_weight(0)
            mask_weight(2)
            lo_weight(1)
            mask_weight(3)
            lo_weight(2)
            text(0)
            lo_weight(3)
            mask_sums(4)
            lo_tile(0, 0)
            mask_sums(5)
            text(1)
            lo_tile(1, 1)
            dve.wait_ge(den_ok, 1)
            V.reciprocal(par[:, 14, 0:N], par[:, 14, 0:N]).then_inc(recip_ok, 1)
            mask_weight(4)
            mask_sums(6)
            mask_weight(5)
            lo_weight(4)
            mask_sums(7)
            mask_weight(6)
            lo_weight(5)
            mask_weight(7)
            lo_weight(6)
            lo_weight(7)
            dve.wait_ge(k_ev, KU)
            turns(0)
            add_rows(0, 0)
            text(2)
            tables(0)
            factors(0, 0)
            lo_tile(2, 2)
            factors(0, 1)
            add_rows(1, 1)
            text(3)
            factors(0, 2)
            lo_tile(3, 3)
            factors(0, 3)
            turns(1)
            add_rows(2, 2)
            normalise(4, 0, h_count(1, 1))
            tables(1)
            factors(1, 0)
            lo_tile(4, 0)
            add_rows(3, 3)

            def part1(m, s, more):
                t = NT * m + s
                normalise(t + 1, (s + 1) % NT, h_count(1, m + (s + 1) // NT))
                if s == 0:
                    factors(m, 1)
                elif s == 1:
                    factors(m, 3)
                elif s == 2 and more:
                    turns(m + 1)
                elif s == 3 and more:
                    tables(m + 1)
                    factors(m + 1, 0)
                lo_tile(t + 1, s + 1)
                if s == 0:
                    factors(m, 2)
                add_rows(t, s)

            OWN_PART1 = 30
            repeat(1, HBLK - 1, OWN_PART1, lambda m: [part1(m, s, True) for s in range(NT)])
            for s in range(NT):
                part1(HBLK - 1, s, False)

            t0 = NT * HBLK
            then(V.tensor_reduce(rank_id[:, :], ident[:, :].rearrange("p (j r) -> p r j", r=RANK), AX.X, ALU.add))
            dve.wait_ge(col_ok, 1)
            then(V.tensor_copy(g_col[:, :, :], side[0][:, 0:NG * NB].rearrange("p (g b) -> p g b", g=NG)))
            V.tensor_tensor(g_mat[:, :, :].rearrange("p g (b r) -> p (g b) r", r=RANK),
                            g_col[:, :, :].rearrange("p g b -> p (g b)").unsqueeze(2)
                            .to_broadcast([P, NG * NB, RANK]),
                            rank_id[:, :].unsqueeze(1).to_broadcast([P, NG * NB, RANK]), ALU.mult)\
             .then_inc(g_ok, 1)
            normalise(t0 + 1, 1, h_count(1, HBLK))
            lo_tile(t0 + 1, 1)
            add_rows(t0, 0)
            for k in range(KC):
                dve.wait_ge(a_hi_ok, k + 1)
                V.tensor_tensor(a_lo[:, k, :, 0:2 * RANK],
                                side[k % 2][:, 0:NB * RANK].rearrange("p (s r) -> p s r", s=NT),
                                a_hi[:, k, :, 0:2 * RANK].bitcast(F32), ALU.subtract)
                V.tensor_tensor(a_lo[:, k, :, 2 * RANK:LR],
                                side[k % 2][:, NB * RANK:(NB + 1) * RANK].unsqueeze(1).to_broadcast([P, NT, RANK]),
                                a_hi[:, k, :, 2 * RANK:LR].bitcast(F32), ALU.subtract).then_inc(a_lo_ok, 1)
            for s in (2, 3):
                normalise(t0 + s, s, h_count(1, HBLK))
                lo_tile(t0 + s, s)
                add_rows(t0 + s - 1, s - 1)
                for k in range((s - 2) * KC // 2, (s - 1) * KC // 2):
                    dve.wait_ge(w2_hi_ok, k + 1)
                    V.tensor_tensor(w2_lo[:, k, :], w2_raw[:, k, :], w2_hi[:, k, :].bitcast(F32), ALU.subtract)\
                     .then_inc(w2_lo_ok, 1)

            normalise(G1, 0, h_count(2, 0))
            lo_tile(G1, 0)
            add_rows(t0 + 3, 3)
            for s in range(NT):
                dve.wait_ge(b_hi_ok, s + 1)
                V.tensor_tensor(b_lo[:, s, :], b_full[:, s, :], b_hi[:, s, :].bitcast(F32), ALU.subtract)\
                 .then_inc(b_lo_ok, 1)
            dve.wait_ge(rows_ok, 1)

            def part2(g, s, more):
                t = G1 + NT * g + s
                dve.wait_ge(ax_ps, t - G1 + 1)
                then(V.tensor_tensor(ax_f[:, :], side[s % 2][0:LR, 0:P], own_rows[:, :], ALU.mult))
                then(V.tensor_tensor(ax_g[:, :], side[s % 2][0:LR, P:2 * P], own_rows[:, :], ALU.mult))
                V.tensor_tensor(ax_f[:, :], ax_f[:, :], ax_g[:, :], ALU.add).then_inc(ax_f_ok, 1)
                dve.wait_ge(ax_hi_ok, t - G1 + 1)
                V.tensor_tensor(ax_lo[s % 2][0:LR, :], ax_f[:, :], ax_hi[s % 2][0:LR, :].bitcast(F32), ALU.subtract)\
                 .then_inc(ax_lo_ok, 1)
                if more:
                    normalise(t + 1, (s + 1) % NT, h_count(2, g + (s + 1) // NT))
                    lo_tile(t + 1, s + 1)
                add_rows(t, s)

            OWN_PART2 = 28
            repeat(0, HBLK, OWN_PART2, lambda g: [part2(g, s, True) for s in range(NT)])
            for s in range(NT):
                part2(HBLK, s, s < NT - 1)

        @block.tensor
        def _(pe):
            mm = nc.tensor.matmul
            pe.wait_ge(const_ok, 1)

            def c_transposes(g):
                pe.wait_ge(dup_ok[g // 4], g % 4 + 1)
                if g >= 2:
                    pe.wait_ge(k_ev, g - 1)
                for j in range(4):
                    c, z = 4 * (g % 4) + j, g // 4
                    ins = nc.tensor.transpose(side[g % 2][:, j * P:(j + 1) * P],
                                              x_dup[:, z, c, :, :].rearrange("h t n -> h (t n)"), ident[:, :])
                ins.then_inc(k_ok, 1)

            def mode_transposes():
                pe.wait_ge(k_ev, 8)
                pe.wait_ge(modes_ok, 1)
                for g, n in ((0, 4), (1, 2)):
                    for j in range(n):
                        ins = nc.tensor.transpose(side[g][:, j * P:(j + 1) * P],
                                                  modes_in[:, 4 * g + j, :, :].rearrange("h z n -> h (z n)"), ident[:, :])
                    ins.then_inc(k_ok, 1)

            def block_sums(i):
                pe.wait_ge(msum_ok, i + 1)
                if i >= 2:
                    pe.wait_ge(mask_ok, i - 1)
                mm(acc[i % 2][:, HALF:HALF + D // 32], blocks[:, :], msum[i % 2][:, :], start=True, stop=True)\
                  .then_inc(bs_ok, 1)

            def transposes(u, src, first=False):
                for b in range(2):
                    if not first:
                        pe.wait_ge(lo_ok, 2 * u - 1 + b)
                    for j in range(4):
                        k = 4 * b + j
                        ins = nc.tensor.transpose(tp[b][:, j * P:(j + 1) * P], src[:, k * P:(k + 1) * P], ident[:, :])
                    ins.then_inc(tp_full, 1)

            def weight_tile(i):
                pe.wait_ge(mask_ok, i + 1)
                transposes(weight_unit(i), w_nat[i % 4], i == 0)

            def split_mm(dst, l_hi, l_lo, r_hi, r_lo, start, stop):
                mm(dst, l_hi, r_hi, start=start, stop=False)
                mm(dst, l_hi, r_lo, start=False, stop=False)
                return mm(dst, l_lo, r_hi, start=False, stop=stop)

            def tile_transposes(t):
                pe.wait_ge(d_ok, t + 1)
                transposes(tile_unit(t), d_t)

            def product(s, chunks, r_hi, r_lo, end, halves=(0, 1)):
                for k in chunks:
                    for half in halves:
                        cols = slice(half * HALF, (half + 1) * HALF)
                        ins = split_mm(acc[s % 2][:, cols], d_hi[s % 2][:, k, :], d_lo[s % 2][:, k, :],
                                       r_hi[:, k, cols], r_lo[:, k, cols], k == 0, end and k == KC - 1)
                return ins

            def begin(t):
                pe.wait_ge(lo_ok, 2 * tile_unit(t) + 2)
                if not (isinstance(t, int) and t < 2):
                    pe.wait_ge(acc_free, t - 1)

            FIRST, SECOND = range(0, KC // 2), range(KC // 2, KC)

            def tile1(t, s, taps=None):
                begin(t)
                product(s, FIRST, w1_hi, w1_lo, True)
                if taps is not None:
                    tap_products(*taps)
                tile_transposes(t + 1)
                product(s, SECOND, w1_hi, w1_lo, True).then_inc(gemm_ok, 1)

            def tap_products(m, s):
                q = NT * m + s
                pe.wait_ge(r_ok, q + 1)
                pe.wait_ge(l_ok, q + 1)
                pe.wait_ge(k_ev, KU + 2 * q)
                for h in range(HS):
                    ins = mm(side[h // 4][:, (h % 4) * STEP:(h % 4 + 1) * STEP],
                             left[s % 2][:, h, :, :].rearrange("p c a -> p (c a)"), right[s % 2][:, h, :],
                             start=True, stop=True)
                    if h % 4 == 3:
                        ins.then_inc(k_ok, 1)

            block_sums(0)
            block_sums(1)
            for i in range(KC // 2):
                weight_tile(i)
                if i < 2:
                    block_sums(i + 2)
            tile_transposes(0)
            begin(0)
            product(0, FIRST, w1_hi, w1_lo, True, (0,))
            block_sums(4)
            block_sums(5)
            tile_transposes(1)
            c_transposes(0)
            c_transposes(1)
            product(0, SECOND, w1_hi, w1_lo, True, (0,))
            begin(1)
            for i, chunks in ((4, FIRST), (5, SECOND), (6, None), (7, None)):
                weight_tile(i)
                if i < 6:
                    block_sums(i + 2)
                    c_transposes(2 * i - 6)
                    c_transposes(2 * i - 5)
                    product(1, chunks, w1_hi, w1_lo, True, (0,))
                elif i == 6:
                    c_transposes(6)
                    c_transposes(7)
            mode_transposes()
            pe.wait_ge(lo_ok, 2 * weight_unit(KC - 1) + 2)
            for k in (FIRST, SECOND):
                ins = product(0, k, w1_hi, w1_lo, True, (1,))
            ins.then_inc(gemm_ok, 1)
            product(1, FIRST, w1_hi, w1_lo, True, (1,))
            tile_transposes(2)
            product(1, SECOND, w1_hi, w1_lo, True, (1,)).then_inc(gemm_ok, 1)
            tap_products(0, 0)
            tile1(2, 2, (0, 1))
            tap_products(0, 2)
            begin(3)
            product(3, range(0, 2), w1_hi, w1_lo, True)
            tap_products(0, 3)
            product(3, range(2, KC // 2), w1_hi, w1_lo, True)
            tile_transposes(4)
            product(3, SECOND, w1_hi, w1_lo, True).then_inc(gemm_ok, 1)

            def block1(m):
                tap_products(m, 0)
                for s in range(NT):
                    tile1(NT * m + s, s, (m, s + 1) if s < NT - 1 else None)

            with pe.Fori(1, HBLK) as m:
                block1(m)

            t0 = NT * HBLK
            pe.wait_ge(sel_ok, 1)
            pe.wait_ge(k_ev, KU + 2 * t0)
            for g in range(NG):
                ins = mm(side[0][:, g * NB:(g + 1) * NB], g_sel[:, g, :], gate_t[:, :], start=True, stop=True)
            ins.then_inc(col_ok, 1)
            tile1(t0, 0)
            pe.wait_ge(g_ok, 1)
            pe.wait_ge(la_in, 32)
            for k in range(KC):
                if k >= 2:
                    pe.wait_ge(a_lo_ok, k - 1)
                cols = slice(k * P, (k + 1) * P)
                for g in range(NG):
                    mm(side[k % 2][:, 0:NB * RANK], a_nat[:, g, cols], g_mat[:, g, :], start=(g == 0), stop=(g == NG - 1))
                nc.tensor.transpose(side[k % 2][:, NB * RANK:(NB + 1) * RANK], as_nat[:, cols], ident[0:RANK, 0:RANK])\
                  .then_inc(a_ps, 1)
            pe.wait_ge(a_lo_ok, KC)
            pe.wait_ge(lb_in, 48)
            for g in range(NG + 1):
                if g < NG:
                    pe.wait_ge(bl_ok, g + 1)
                for b in range(2):
                    n = 2 * g + b
                    if n >= 2:
                        pe.wait_ge(bt_ev, n - 1)
                    for j in range(4):
                        c = 4 * b + j
                        if g < NG:
                            ins = nc.tensor.transpose(side[b][:, j * P:(j + 1) * P],
                                                      bl_by_o[:, g, c, :, :].rearrange("p n r -> p (n r)"), ident[:, :])
                        else:
                            ins = nc.tensor.transpose(side[b][0:RANK, j * P:(j + 1) * P], bs_nat[:, c, :], ident[:, :])
                    ins.then_inc(bt_ps, 1)
            pe.wait_ge(bt_ev, 2 * NG + 2)
            for j in range(4):
                half, quad = j // 2, j % 2
                if j >= 2:
                    pe.wait_ge(bm_ev, j - 1)
                for g in range(NG):
                    ins = mm(side[j % 2][:, :], g_mat[:, g, quad * P:(quad + 1) * P],
                             b_tr[:, g, half * HALF:(half + 1) * HALF], start=(g == 0), stop=(g == NG - 1))
                ins.then_inc(bm_ps, 1)
            for s in range(1, NT):
                tile1(t0 + s, s)

            pe.wait_ge(bm_ev, 4)
            pe.wait_ge(w2_lo_ok, KC)

            def down(t, s):
                for k in range(KC):
                    both = d_hl[s % 2][:, k, :, :].rearrange("p z r -> p (z r)")
                    mm(side[s % 2][0:LR, 0:2 * P], a_hi[:, k, s, :], both, start=(k == 0), stop=False)
                    ins = mm(side[s % 2][0:LR, 0:2 * P], a_lo[:, k, s, :], both, start=False, stop=(k == KC - 1))
                ins.then_inc(ax_ps, 1)

            def up(t, s):
                pe.wait_ge(ax_lo_ok, t - G1 + 1)
                for half in range(2):
                    cols = slice(half * HALF, (half + 1) * HALF)
                    ins = split_mm(acc[s % 2][:, cols], ax_hi[s % 2][:, :], ax_lo[s % 2][:, :],
                                   b_hi[:, s, cols], b_lo[:, s, cols], False, True)
                return ins

            def tile2(g, s, more, first=False):
                t = G1 + NT * g + s
                begin(t)
                down(t, s)
                product(s, range(0, KC // 2), w2_hi, w2_lo, False)
                if more:
                    tile_transposes(t + 1)
                product(s, range(KC // 2, KC), w2_hi, w2_lo, False)
                if first:
                    pe.wait_ge(b_lo_ok, NT)
                up(t, s).then_inc(gemm_ok, 1)

            for s in range(NT):
                tile2(0, s, True, first=s == 0)
            with pe.Fori(1, HBLK) as g:
                for s in range(NT):
                    tile2(g, s, True)
            for s in range(NT):
                tile2(HBLK, s, s < NT - 1)


_INS = ['x', 'txt', 'L0_tok_log_dt', 'L0_tok_B', 'L0_tok_inv_A_real', 'L0_tok_A_imag', 'L0_attn_weight',
        'L0_attn_mask', 'L0_ffn_gate', 'L0_ffn_kernel', 'L0_ffn_bias', 'L0_ffn_lora_A', 'L0_ffn_lora_B',
        'L0_ffn_lora_A_shared', 'L0_ffn_lora_B_shared']
_OUTS = [((16, 160, 1024), 'float32')]


def kernel(**inputs):
    import numpy as _np
    import concourse.bacc as _bacc
    from concourse import mybir as _mybir
    from concourse.bass_utils import run_bass_kernel_spmd as _run

    nc = _bacc.Bacc("TRN2", target_bir_lowering=False, num_devices=1)
    arrays, args = {}, []
    for name in _INS:
        a = _np.ascontiguousarray(inputs[name])
        arrays[f"in_{name}_dram"] = a
        args.append(nc.dram_tensor(f"in_{name}_dram", a.shape, _mybir.dt.from_np(a.dtype), kind="ExternalInput").ap())
    for i, (shape, dtype) in enumerate(_OUTS):
        dt = _mybir.dt.from_np(_np.dtype(dtype))
        args.append(nc.dram_tensor(f"out_{i}_dram", shape, dt, kind="ExternalOutput").ap())
    build_fusion_layer(nc, *args)
    r = _run(nc, [arrays], core_ids=[0])
    got = tuple(r.results[0][f"out_{i}_dram"] for i in range(len(_OUTS)))
    return got[0]
```

```python
import math
from contextlib import ExitStack

import concourse.bass as bass
from concourse import mybir


def build_fusion_layer(
    nc: bass.Bass,
    x: bass.AP,
    txt: bass.AP,
    log_dt: bass.AP,
    B: bass.AP,
    inv_A_real: bass.AP,
    A_imag: bass.AP,
    attn_w: bass.AP,
    attn_mask: bass.AP,
    gate: bass.AP,
    ffn_w: bass.AP,
    bias: bass.AP,
    lora_A: bass.AP,
    lora_B: bass.AP,
    lora_A_shared: bass.AP,
    lora_B_shared: bass.AP,
    out: bass.AP,
):
    F32, F32R, I32 = mybir.dt.float32, mybir.dt.float32r, mybir.dt.int32
    ALU, ACT, AX = mybir.AluOpType, mybir.ActivationFunctionType, mybir.AxisListType

    P = 128
    CH, H, N, _ = x.shape
    _, TXT, D = txt.shape
    ROWS = H + TXT
    NB, NLORA = gate.shape
    RANK = lora_A.shape[1]
    KC = D // P
    HALF = D // 2
    GR = 32
    NT = CH * GR // P
    CPT = CH // NT
    HBLK = H // GR
    GROUPS = HBLK + 1
    STEP, NA = P, D // P
    NB0, NB1 = 8, 16
    HS = GR // NT
    NE = NB0 + NB1 + NA
    GP = P // RANK
    NG = NLORA // GP
    LR = 3 * RANK
    LK = LR + 1
    OPB = D // P
    EPS = 1e-5
    MAGIC = 1.5 * 2.0 ** 23
    TWO_PI = 6.283185
    PI_1, PI_2, PI_3 = 6.28125, 1.93500518798828125e-3, 3.0199157663e-7
    LN2_HI, LN2_LO = 0.693359375, -2.12194440e-4

    taps = nc.dram_tensor("taps", [H, CH, D], F32, kind="Internal").ap()
    mid = nc.dram_tensor("mid", [GROUPS, NT, P, D], F32, kind="Internal").ap()

    ctx = ExitStack()
    with ctx:
        def sem(name):
            return ctx.enter_context(nc.semaphore(name))

        KB = 1024
        base = 16512
        at = {"end": base}

        def place(name, shape, dt, offset):
            size = 4
            for n in shape[1:]:
                size *= n
            at["end"] = offset + size
            return nc.alloc_sbuf_tensor_at(name, shape, dt, offset=offset)

        def after(name, shape, dt):
            return place(name, shape, dt, (at["end"] + 31) // 32 * 32)

        W0 = base
        w1_hi = place("w1_hi", [P, KC, D], F32R, W0)
        w1_lo = after("w1_lo", [P, KC, D], F32R)
        b_hi = place("b_hi", [LK, NT, D], F32R, W0)
        b_lo = after("b_lo", [LK, NT, D], F32R)
        S0 = W0 + 64 * KB
        c_re = place("c_re", [P, H, CH], F32, S0)
        c_im = after("c_im", [P, H, CH], F32)
        modes = after("modes", [P, 6, H], F32)
        turn = after("turn", [P, GR, NE], F32)
        mag = after("mag", [P, GR, NE], F32)
        decay = after("decay", [P, GR, NE], F32)
        SN = 2 * NB0 + 2 * NB1 + 3 * NA
        wave = after("wave", [P, GR, SN], F32)
        fdec = after("fdec", [P, 2, GR, NA], F32)
        lead = after("lead", [P, 2, GR, NA], F32)
        lead2 = after("lead2", [P, 2, GR, NA], F32)
        right = [after(f"right{i}", [P, HS, STEP], F32) for i in range(2)]
        left = [after(f"left{i}", [P, HS, CH, NA], F32) for i in range(2)]
        ST = at["end"]
        rtmp = after("rtmp", [P, HS, STEP], F32)
        ltmp = after("ltmp", [P, HS, CH, NA], F32)
        SK = at["end"]
        kst = [after(f"kst{i}", [P, HS, STEP], F32) for i in range(2)]
        assert at["end"] <= S0 + 80 * KB, at["end"] - S0
        x_nat = place("x_nat", [P, CH, N, 2], F32, ST)
        x_dup = place("x_dup", [P, 2, CH, 2, N], F32, S0 + 31 * KB)
        modes_in = place("modes_in", [P, 6, 2, N], F32, S0 + 55 * KB)
        XW = N + 1
        par = place("par", [P, 24, XW], F32, SK)
        pint = after("pint", [P, XW], I32)
        b_nat = after("b_nat", [P, N, 2], F32)
        a_nat = place("a_nat", [P, NG, D], F32, S0)
        bl_by_o = place("bl_by_o", [P, NG, OPB, GP, RANK], F32, S0)
        bl_nat = after("bl_nat", [P, NLORA, OPB, RANK], F32)
        b_tr = after("b_tr", [P, NG, D], F32)
        g_mat = after("g_mat", [P, NG, NB * RANK], F32)
        as_nat = after("as_nat", [RANK, D], F32)
        bs_nat = after("bs_nat", [P, OPB, RANK], F32)
        g_sel = after("g_sel", [NLORA, NG, P], F32)
        g_col = after("g_col", [P, NG, NB], F32)
        gate_t = after("gate_t", [NLORA, NB], F32)
        assert at["end"] <= S0 + 64 * KB
        w2_hi = place("w2_hi", [P, KC, D], F32R, S0)
        w2_lo = after("w2_lo", [P, KC, D], F32R)
        w2_raw = place("w2_raw", [P, KC, D], F32, S0 + 32 * KB)
        b_full = place("b_full", [LK, NT, D], F32, S0 + 64 * KB)
        A0 = S0 + 80 * KB
        w_nat = [place(f"w_nat{i}", [P, D], F32, at_) for i, at_ in
                 enumerate((A0, A0 + 4 * KB, A0 + 8 * KB, S0 + 47 * KB))]
        m_nat = [place(f"m_nat{i}", [P, D], I32, at_) for i, at_ in
                 enumerate((A0 + 12 * KB, A0 + 16 * KB, A0 + 20 * KB, S0 + 51 * KB))]
        a_hi = place("a_hi", [P, KC, NT, LR], F32R, A0)
        a_lo = after("a_lo", [P, KC, NT, LR], F32R)
        h_t = [place("h_t0", [P, D], F32, A0 + 24 * KB)] + [after(f"h_t{i}", [P, D], F32) for i in (1, 2, 3)]
        d_t = after("d_t", [P, D], F32)
        d_hl = [after(f"d_hl{i}", [P, KC, 2, P], F32R) for i in range(2)]
        d_hi, d_lo = ([d[:, :, z, :] for d in d_hl] for z in range(2))
        ident = after("ident", [P, P], F32)
        blocks = after("blocks", [P, P], F32)
        msum = [after(f"msum{i}", [P, D // 32], F32) for i in range(2)]
        etab = after("etab", [P, 2, NE], F32)
        half_pi = after("half_pi", [P, 2], F32)
        stat = after("stat", [P, 2, 6], F32)
        mv = after("mv", [P, 2], F32)
        sc = after("sc", [P, 8], F32)
        assert at["end"] <= 229368, at["end"]
        etab_i = place("etab_i", [P, 2, NE], I32, SK + 7 * KB + 512)
        rank_id = place("rank_id", [P, RANK], F32, S0 + 63 * KB)
        own_rows = place("own_rows", [LR, P], F32, W0 + 32 * KB)
        ax_f = after("ax_f", [LR, P], F32)
        ax_g = after("ax_g", [LR, P], F32)
        ax_hi = [after(f"ax_hi{i}", [LK, P], F32R) for i in range(2)]
        ax_lo = [after(f"ax_lo{i}", [LK, P], F32R) for i in range(2)]

        def banks(name, n):
            return ctx.enter_context(nc.psum_tensor(name, [P, n * HALF], F32))

        acc = [banks(f"acc{i}", 2) for i in range(2)]
        tp = [banks(f"tp{i}", 1) for i in range(2)]
        side = [banks(f"side{i}", 1) for i in range(2)]

        dup_ok = sem("dup_ok")
        bl_ok = sem("bl_ok")
        const_ok = sem("const_ok")
        par_in = sem("par_in")
        x_in = sem("x_in")
        w_in = [sem(f"w_in{i}") for i in range(4)]
        h_in = [sem(f"h_in{i}") for i in range(4)]
        h_out = [sem(f"h_out{i}") for i in range(4)]
        own = sem("own")
        own_pool = sem("own_pool")
        exp_ok, den_ok, recip_ok = sem("exp_ok"), sem("den_ok"), sem("recip_ok")
        etab_ok, turn0_ok = sem("etab_ok"), sem("turn0_ok")
        whole0_ok = sem("whole0_ok")
        turn1_ok, sin1_ok = sem("turn1_ok"), sem("sin1_ok")
        modes_ok, msum_ok = sem("modes_ok"), sem("msum_ok")
        bs_ok, mask_ok = sem("bs_ok"), sem("mask_ok")
        acc_free = sem("acc_free")
        tp_full = sem("tp_full")
        hi_ok = sem("hi_ok")
        lo_ok = sem("lo_ok")
        var_ok, sd_ok = sem("var_ok"), sem("sd_ok")
        d_ok = sem("d_ok")
        gemm_ok = sem("gemm_ok")
        tab_ok, wave_ok = sem("tab_ok"), sem("wave_ok")
        lead_ok, ltmp_ok = sem("lead_ok"), sem("ltmp_ok")
        rmul_ok, lmul_ok = sem("rmul_ok"), sem("lmul_ok")
        r_ok, l_ok = sem("r_ok"), sem("l_ok")
        k_ok, k_ev = sem("k_ok"), sem("k_ev")
        k_out = [sem(f"k_out{i}") for i in range(4)]
        gate_in = sem("gate_in")
        la_in, lb_in = sem("la_in"), sem("lb_in")
        sel_ok, col_ok, g_ok = sem("sel_ok"), sem("col_ok"), sem("g_ok")
        a_ps, a_hi_ok, a_lo_ok = sem("a_ps"), sem("a_hi_ok"), sem("a_lo_ok")
        bt_ps, bt_ev = sem("bt_ps"), sem("bt_ev")
        bm_ps, bm_ev = sem("bm_ps"), sem("bm_ev")
        w2_in, w2_hi_ok, w2_lo_ok = sem("w2_in"), sem("w2_hi_ok"), sem("w2_lo_ok")
        rows_ok = sem("rows_ok")
        b_hi_ok, b_lo_ok = sem("b_hi_ok"), sem("b_lo_ok")
        ax_ps, ax_f_ok, ax_hi_ok, ax_lo_ok = sem("ax_ps"), sem("ax_f_ok"), sem("ax_hi_ok"), sem("ax_lo_ok")

        WU = KC
        UNITS = ["w0", "w1", "t0", "w2", "w3", "t1", "w4", "w5", "w6", "w7"]

        def tile_unit(t):
            return UNITS.index(f"t{t}") if isinstance(t, int) and t < 2 else WU + t

        def weight_unit(i):
            return UNITS.index(f"w{i}")

        G1 = GROUPS * NT
        KU = 10

        def h_count(phase, m):
            if phase == 1:
                return 64 * m + 16
            return 64 * HBLK + 32 + 16 * m

        block = ctx.enter_context(nc.Block())

        @block.sync
        def _(sp):
            def load_w(i):
                sp.dma_start(m_nat[i % 4][:, :], attn_mask[i * P:(i + 1) * P, :]).then_inc(w_in[i % 4], 16)
                sp.dma_start(w_nat[i % 4][:, :], attn_w[i * P:(i + 1) * P, :]).then_inc(w_in[i % 4], 16)

            def load_text(s):
                sp.dma_start(h_t[s][:, :], txt[CPT * s:CPT * (s + 1), :, :].rearrange("c t d -> (c t) d"))\
                  .then_inc(h_in[s], 16)

            sp.dma_start(par[:, 0, 0:N], A_imag).then_inc(par_in, 16)
            sp.dma_start(par[:, 1, 0:N], inv_A_real).then_inc(par_in, 16)
            sp.dma_start(par[:, 1, N:XW], log_dt.rearrange("(h o) -> h o", o=1)).then_inc(par_in, 16)
            sp.dma_start(b_nat[:, :, :], B).then_inc(par_in, 16)
            load_w(0)
            load_w(1)
            load_text(0)
            load_w(2)
            load_w(3)
            sp.dma_start(x_nat[:, :, :, :], x.rearrange("c h n z -> h c n z")).then_inc(x_in, 16)
            load_text(1)
            for i in range(4, KC):
                sp.wait_ge(msum_ok, i - 3)
                sp.wait_ge(tp_full, 2 * weight_unit(i - 4) + 2)
                load_w(i)
            load_text(2)
            load_text(3)

            def store_taps(m, s):
                sp.wait_ge(k_ev, KU + 2 * (NT * m + s) + 2)
                sp.dma_start(taps[bass.ds(GR * m + HS * s, HS), :, :].rearrange("h c (a b) -> (c a) h b", b=STEP),
                             kst[s % 2][:, :, :]).then_inc(k_out[s], 16)

            def store_mid(m, s):
                sp.wait_ge(acc_free, NT * m + s + 1)
                sp.dma_start(mid[bass.ds(m, 1), s, :, :].rearrange("o p d -> (o p) d"), h_t[s][:, :])\
                  .then_inc(h_out[s], 16)

            def load_block(m, s):
                sp.wait_ge(h_out[s], 16 * (m + 1))
                for c in range(CPT):
                    sp.dma_start(h_t[s][c * GR:(c + 1) * GR, :],
                                 taps[bass.ds(GR * m, GR), CPT * s + c, :]).then_inc(h_in[s], 16)

            def load_mid(g, slot, s):
                sp.dma_start(h_t[s][:, :], mid[bass.ds(slot, 1), s, :, :].rearrange("o p d -> (o p) d"))\
                  .then_inc(h_in[s], 16)

            def block_io(m, lora):
                first = isinstance(m, int) and m == 0
                if first:
                    store_mid(m, 0)
                store_taps(m, 0)
                if first:
                    store_mid(m, 1)
                if not first:
                    store_mid(m, 0)
                store_taps(m, 1)
                store_taps(m, 2)
                store_mid(m, 2 if first else 1)
                store_taps(m, 3)
                for s in range(NT):
                    sp.wait_ge(k_out[s], 16 * (m + 1))
                for s in range(NT - 2):
                    load_block(m, s)
                if lora:
                    sp.dma_start(gate_t[:, :], gate.rearrange("b n -> n b"),
                                 allow_slow_non_contiguous=True).then_inc(gate_in, 16)
                    sp.dma_start(a_nat[:, :, :], lora_A.rearrange("(g n) r i -> (n r) g i", n=GP)).then_inc(la_in, 16)
                    sp.dma_start(as_nat[:, :], lora_A_shared).then_inc(la_in, 16)
                    sp.dma_start(bl_nat[:, :, :, :], lora_B.rearrange("n (p c) r -> p n c r", c=OPB)).then_inc(lb_in, 16)
                    sp.dma_start(bs_nat[:, :, :], lora_B_shared.rearrange("(p c) r -> p c r", c=OPB)).then_inc(lb_in, 16)
                    sp.dma_start(b_full[LR:LK, :, :], bias.rearrange("(o n) -> o n", o=1).unsqueeze(1)
                                 .to_broadcast([1, NT, D])).then_inc(lb_in, 16)
                if not first:
                    store_mid(m, NT - 2)
                load_block(m, NT - 2)
                store_mid(m, NT - 1)
                load_block(m, NT - 1)

            block_io(0, False)
            with sp.Fori(1, HBLK - 1) as m:
                block_io(m, False)
            block_io(HBLK - 1, True)

            last = HBLK
            store_mid(last, 0)
            store_mid(last, 1)
            sp.wait_ge(h_out[0], 16 * GROUPS)
            load_mid(0, 1, 0)
            sp.wait_ge(bm_ev, 4)
            sp.dma_start(w2_raw[:, :, :], ffn_w.rearrange("(k p) n -> p k n", p=P)).then_inc(w2_in, 16)
            for s in range(2, NT):
                store_mid(last, s)
                sp.wait_ge(h_out[s - 1], 16 * GROUPS)
                load_mid(0, 1, s - 1)
            sp.wait_ge(h_out[NT - 1], 16 * GROUPS)
            load_mid(0, 1, NT - 1)

            def store_out(g, s):
                sp.wait_ge(acc_free, G1 + NT * g + s + 1)
                for c in range(CPT):
                    sp.dma_start(out[CPT * s + c, bass.ds(GR * g, GR), :], h_t[s][c * GR:(c + 1) * GR, :])\
                      .then_inc(h_out[s], 16)

            def next_in(g, slot, s):
                sp.wait_ge(h_out[s], 16 * GROUPS + 64 * (g + 1))
                load_mid(g + 1, slot, s)

            def group_io(g, slot):
                for s in range(NT):
                    store_out(g, s)
                    if s:
                        next_in(g, slot, s - 1)
                next_in(g, slot, NT - 1)

            with sp.Fori(0, HBLK - 1) as g:
                group_io(g, g + 2)
            group_io(HBLK - 1, 0)
            for s in range(NT):
                store_out(HBLK, s)
            for s in range(NT):
                sp.wait_ge(h_out[s], 16 * GROUPS + 64 * GROUPS)

        def exp_parts(e, then, fused, src, w, k, r, p, two_k):
            then(e.tensor_scalar(k, src, 1.0 / math.log(2.0), MAGIC, ALU.mult, ALU.add))
            then(e.tensor_scalar(k, k, MAGIC, None, ALU.subtract))
            fused(r, k, -LN2_HI, src, ALU.mult, ALU.add, w)
            fused(r, k, -LN2_LO, r, ALU.mult, ALU.add, w)
            then(e.tensor_scalar(p, r, 1.0 / math.factorial(7), None, ALU.mult))
            for n in range(6, 0, -1):
                fused(p, p, 1.0 / math.factorial(n), r, ALU.add, ALU.mult, w)
            then(e.tensor_scalar(two_k, k, 127.0, 2.0 ** 23, ALU.add, ALU.mult))

        def over_e(ap, n):
            return ap.unsqueeze(2).to_broadcast([P, GR, n])

        def over_h(ap, n):
            return ap.unsqueeze(1).to_broadcast([P, GR, n])

        def raw_turns(e, m):
            for j, e0, n in ((0, 0, NB0), (1, NB0, NB1), (2, NB0 + NB1, NA)):
                ins = e.tensor_tensor(turn[:, :, e0:e0 + n], over_e(modes[:, j, bass.ds(GR * m, GR)], n),
                                      over_h(etab[:, 0, e0:e0 + n], n), ALU.mult)
            return ins

        def exponents(e, m):
            return e.tensor_tensor(decay[:, :, :], over_e(modes[:, 3, bass.ds(GR * m, GR)], NE),
                                   over_h(etab[:, 1, :], NE), ALU.mult)

        @block.gpsimd
        def _(pool):
            n_own = [0]

            def then(ins):
                n_own[0] += 1
                ins.then_inc(own_pool, 1)
                pool.wait_ge(own_pool, n_own[0])

            nc.gpsimd.memset(blocks[:, :], 0.0).then_inc(own_pool, 1)
            nc.gpsimd.memset(half_pi[:, 0:1], math.pi / 2)
            nc.gpsimd.memset(half_pi[:, 1:2], -math.pi / 2)
            n_own[0] += 1
            then(nc.gpsimd.memset(ident[:, :], 0.0))
            for q in range(P // 32):
                then(nc.gpsimd.memset(blocks[32 * q:32 * (q + 1), 32 * q:32 * (q + 1)], 1.0))
            parts = ((0, NB0, 1), (NB0, NB1, NB0), (NB0 + NB1, NA, STEP))
            for e0, n, l in parts:
                nc.gpsimd.iota(etab_i[:, 0, e0:e0 + n], [[1, n]], base=0, channel_multiplier=0)
                nc.gpsimd.iota(etab_i[:, 1, e0:e0 + n], [[l, n]], base=0, channel_multiplier=0)
            nc.gpsimd.affine_select(out=ident[:, :], in_=ident[:, :], compare_op=ALU.not_equal, fill=1.0,
                                    base=0, pattern=[[-1, P]], channel_multiplier=1).then_inc(const_ok, 1)

            G = nc.gpsimd
            A = lambda j: par[:, j, 0:N]

            def fused(dst, a, scalar, b, op0, op1, w=N):
                then(G.tensor_scalar(par[:, 20, 0:w], a, scalar, None, op0))
                then(G.tensor_tensor(dst, par[:, 20, 0:w], b, op1))

            def wrap(dst, src, tmp):
                then(G.tensor_scalar(tmp, src, MAGIC, MAGIC, ALU.add, ALU.subtract))
                then(G.tensor_tensor(dst, src, tmp, ALU.subtract))

            pool.wait_ge(exp_ok, 1)
            dt = par[:, 8, N:XW]
            then(G.tensor_tensor(A(14), A(8), A(8), ALU.mult))
            then(G.tensor_tensor(A(15), A(0), A(0), ALU.mult))
            G.tensor_tensor(A(14), A(14), A(15), ALU.add).then_inc(den_ok, 1)
            then(G.tensor_scalar(A(9), A(8), dt, -1.0, ALU.mult, ALU.mult))
            then(G.tensor_scalar(A(10), A(0), dt, None, ALU.mult))
            then(G.tensor_scalar(A(5), A(10), 1.0 / (2 * math.pi), MAGIC, ALU.mult, ALU.add))
            then(G.tensor_scalar(A(5), A(5), MAGIC, None, ALU.subtract))
            for part in (PI_1, PI_2, PI_3):
                fused(A(10), A(5), -part, A(10), ALU.mult, ALU.add)
            then(G.tensor_scalar(A(6), A(10), 1.0 / (2 * math.pi), None, ALU.mult))
            wrap(A(4), A(6), A(5))
            G.tensor_copy(modes_in[:, 0, 0, :], A(4)).then_inc(turn1_ok, 1)
            for j, mul in ((1, NB0), (2, STEP)):
                then(G.tensor_scalar(A(6), A(4), float(mul), None, ALU.mult))
                wrap(modes_in[:, j, 0, :], A(6), A(5))
            G.tensor_copy(modes_in[:, 3, 0, :], A(9))
            exp_parts(G, then, fused, A(9), N, A(5), A(6), A(7), pint[:, 0:N])
            tk = pint[:, 0:N].bitcast(F32)
            then(G.tensor_tensor(A(11), A(7), tk, ALU.mult))
            fused(A(11), tk, -1.0, A(11), ALU.add, ALU.add)
            pool.wait_ge(sin1_ok, 1)
            fused(A(12), A(3), -2.0, A(3), ALU.mult, ALU.mult)
            fused(A(12), A(11), 1.0, A(12), ALU.add, ALU.mult)
            then(G.tensor_tensor(A(12), A(12), A(11), ALU.add))
            fused(A(13), A(11), 1.0, A(2), ALU.add, ALU.mult)
            pool.wait_ge(recip_ok, 1)
            then(G.tensor_tensor(A(15), A(13), A(0), ALU.mult))
            then(G.tensor_tensor(A(16), A(12), A(8), ALU.mult))
            then(G.tensor_tensor(A(15), A(15), A(16), ALU.subtract))
            fused(A(15), A(15), 2.0, A(14), ALU.mult, ALU.mult)
            then(G.tensor_tensor(A(16), A(13), A(8), ALU.mult))
            then(G.tensor_tensor(A(17), A(12), A(0), ALU.mult))
            then(G.tensor_tensor(A(16), A(16), A(17), ALU.add))
            fused(A(16), A(16), -2.0, A(14), ALU.mult, ALU.mult)
            b_re, b_im = b_nat[:, :, 0], b_nat[:, :, 1]
            then(G.tensor_tensor(A(17), b_re, A(15), ALU.mult))
            then(G.tensor_tensor(A(18), b_im, A(16), ALU.mult))
            then(G.tensor_tensor(modes_in[:, 4, 0, :], A(17), A(18), ALU.subtract))
            then(G.tensor_tensor(A(17), b_re, A(16), ALU.mult))
            then(G.tensor_tensor(A(18), b_im, A(15), ALU.mult))
            then(G.tensor_tensor(modes_in[:, 5, 0, :], A(17), A(18), ALU.add))
            G.tensor_copy(modes_in[:, :, 1, :], modes_in[:, :, 0, :]).then_inc(modes_ok, 1)

            pool.wait_ge(k_ev, 4)
            pool.wait_ge(etab_ok, 1)
            raw_turns(G, 0).then_inc(turn0_ok, 1)
            exponents(G, 0).then_inc(turn0_ok, 1)
            pool.wait_ge(whole0_ok, 1)
            G.tensor_tensor(turn[:, :, :], turn[:, :, :], mag[:, :, :], ALU.subtract).then_inc(turn0_ok, 1)

            def add_factors(m, s):
                q = NT * m + s
                if s == 0:
                    pool.wait_ge(lead_ok, m + 1)
                if not (isinstance(q, int) and q == 0):
                    pool.wait_ge(l_ok, q)
                G.tensor_tensor(ltmp[:, :, :, :],
                                c_im[:, bass.ds(GR * m + HS * s, HS), :].unsqueeze(3).to_broadcast([P, HS, CH, NA]),
                                lead[:, 1, HS * s:HS * (s + 1), :].unsqueeze(2).to_broadcast([P, HS, CH, NA]),
                                ALU.mult).then_inc(ltmp_ok, 1)
                pool.wait_ge(rmul_ok, q + 1)
                G.tensor_tensor(right[s % 2][:, :, :], right[s % 2][:, :, :], rtmp[:, :, :], ALU.add)\
                 .then_inc(r_ok, 1)
                if isinstance(m, int) and m == 0:
                    return
                pool.wait_ge(lmul_ok, q + 1)
                pool.wait_ge(ltmp_ok, q + 1)
                G.tensor_tensor(left[s % 2][:, :, :, :], left[s % 2][:, :, :, :], ltmp[:, :, :, :], ALU.add)\
                 .then_inc(l_ok, 1)

            for s in range(NT):
                add_factors(0, s)
            with pool.Fori(1, HBLK) as m:
                for s in range(NT):
                    add_factors(m, s)

            pool.wait_ge(gate_in, 16)
            then(nc.gpsimd.memset(g_sel[:, :, :], 0.0))
            nc.gpsimd.affine_select(out=g_sel[:, :, :].rearrange("n g (j r) -> n g j r", r=RANK),
                                    in_=g_sel[:, :, :].rearrange("n g (j r) -> n g j r", r=RANK),
                                    compare_op=ALU.not_equal, fill=1.0, base=0,
                                    pattern=[[-GP, NG], [-1, GP], [0, RANK]], channel_multiplier=1)\
              .then_inc(sel_ok, 1)

            pool.wait_ge(lb_in, 48)
            pool.wait_ge(a_ps, KC)
            for g in range(NG):
                nc.gpsimd.tensor_copy(bl_by_o[:, g, :, :, :],
                                      bl_nat[:, GP * g:GP * (g + 1), :, :].rearrange("p n c r -> p c n r"))\
                  .then_inc(bl_ok, 1)

            pool.wait_ge(gemm_ok, G1)
            then(nc.gpsimd.memset(own_rows[2 * RANK:LR, :], 1.0))
            then(nc.gpsimd.memset(own_rows[0:2 * RANK, :], 0.0))
            for i in range(2):
                then(nc.gpsimd.memset(ax_hi[i][LR:LK, :].bitcast(F32), 1.0))
                then(nc.gpsimd.memset(ax_lo[i][LR:LK, :].bitcast(F32), 0.0))
            then(nc.gpsimd.memset(own_rows[0:RANK, 0:P // 2], 1.0))
            nc.gpsimd.memset(own_rows[RANK:2 * RANK, P // 2:P], 1.0).then_inc(rows_ok, 1)

        @block.scalar
        def _(act):
            def hi_unit(u, dst):
                for b in range(2):
                    act.wait_ge(tp_full, 2 * u + b + 1)
                    nc.scalar.activation(dst[:, 4 * b:4 * b + 4, :],
                                         tp[b][:, :].rearrange("p (k r) -> p k r", k=4), ACT.Copy)\
                      .then_inc(hi_ok, 1)

            def hi_tile(t, s):
                if not (isinstance(t, int) and t < 2):
                    act.wait_ge(gemm_ok, t - 1)
                hi_unit(tile_unit(t), d_hi[s % 2])

            def std(t):
                act.wait_ge(var_ok, t + 1)
                nc.scalar.activation(sc[:, 1:2], sc[:, 0:1], ACT.Sqrt).then_inc(sd_ok, 1)

            def decays():
                nc.scalar.activation(decay[:, :, :], decay[:, :, :], ACT.Exp)

            def waves(m):
                act.wait_ge(tab_ok, m + 1)
                if not (isinstance(m, int) and m == 0):
                    act.wait_ge(rmul_ok, NT * m)
                    decays()
                re, im = slice(0, N), slice(N, P)

                def put(part, w0, n, e0, form):
                    src = mag if form.endswith("cos") else turn
                    scale = {"cos": -TWO_PI, "-cos": TWO_PI, "sin": TWO_PI, "-sin": -TWO_PI}[form]
                    bias_ap = {"cos": half_pi[part, 0:1], "-cos": half_pi[part, 1:2]}.get(form, 0.0)
                    return nc.scalar.activation(wave[part, :, w0:w0 + n], src[part, :, e0:e0 + n], ACT.Sin,
                                                bias=bias_ap, scale=scale)

                put(re, 0, NB0, 0, "cos")
                put(im, 0, NB0, 0, "sin")
                put(re, NB0, NB0, 0, "sin")
                put(im, NB0, NB0, 0, "cos")
                w0, e0 = 2 * NB0, NB0
                put(slice(0, P), w0, NB1, e0, "cos")
                put(re, w0 + NB1, NB1, e0, "-sin")
                put(im, w0 + NB1, NB1, e0, "sin")
                w0, e0 = 2 * NB0 + 2 * NB1, NB0 + NB1
                put(re, w0, NA, e0, "cos")
                put(im, w0, NA, e0, "-sin")
                put(re, w0 + NA, NA, e0, "-sin")
                put(im, w0 + NA, NA, e0, "-cos")
                put(re, w0 + 2 * NA, NA, e0, "-cos")
                put(im, w0 + 2 * NA, NA, e0, "sin").then_inc(wave_ok, 1)

            def taps_out(m, s):
                if s >= 2:
                    act.wait_ge(k_out[s - 2], 16 * (m + 1))
                for b in range(2):
                    act.wait_ge(k_ok, KU + 2 * (NT * m + s) + b + 1)
                    nc.scalar.activation(kst[s % 2][:, 4 * b:4 * b + 4, :],
                                         side[b][:, :].rearrange("p (h b) -> p h b", b=STEP), ACT.Copy)\
                      .then_inc(k_ev, 1)

            def modes_out():
                for g in range(2):
                    act.wait_ge(k_ok, 2 + g + 1)
                    n = (4, 2)[g]
                    nc.scalar.activation(modes[:, 4 * g:4 * g + n, :],
                                         side[g][:, 0:n * P].rearrange("p (j h) -> p j h", j=n), ACT.Copy)\
                      .then_inc(k_ev, 1)

            def double(z, g):
                nc.scalar.copy(x_dup[:, z, 4 * g:4 * g + 4, :, :],
                               x_nat[:, 4 * g:4 * g + 4, :, z].unsqueeze(2).to_broadcast([P, 4, 2, N]))\
                  .then_inc(dup_ok, 1)

            def hi_weight(i):
                hi_unit(weight_unit(i), w1_hi[:, :, i * P:(i + 1) * P])

            def c_out(g):
                act.wait_ge(k_ok, (g if g < 2 else g + 2) + 1)
                dst = (c_re, c_im)[g // 4]
                nc.scalar.activation(dst[:, :, 4 * (g % 4):4 * (g % 4) + 4],
                                     side[g % 2][:, :].rearrange("p (c h) -> p h c", c=4), ACT.Copy)\
                  .then_inc(k_ev, 1)

            hi_weight(0)
            std(0)
            hi_weight(1)
            hi_tile(0, 0)
            hi_weight(2)
            hi_weight(3)
            act.wait_ge(turn1_ok, 1)
            nc.scalar.activation(par[:, 2, 0:N], par[:, 4, 0:N], ACT.Sin, scale=TWO_PI)
            nc.scalar.activation(par[:, 3, 0:N], par[:, 4, 0:N], ACT.Sin, scale=TWO_PI / 2).then_inc(sin1_ok, 1)
            act.wait_ge(x_in, 16)
            for g in range(4):
                double(0, g)
            std(1)
            hi_tile(1, 1)
            for g in range(4):
                double(1, g)
            for i in range(KC // 2, KC):
                if i == KC // 2 + 1:
                    modes_out()
                if i == KC - 1:
                    std(2)
                c_out(2 * i - KC)
                c_out(2 * i - KC + 1)
                if i == KC - 1:
                    act.wait_ge(turn0_ok, 2)
                    decays()
                hi_weight(i)
            waves(0)
            std(3)
            hi_tile(2, 2)
            taps_out(0, 0)
            hi_tile(3, 3)
            taps_out(0, 1)
            taps_out(0, 2)
            taps_out(0, 3)
            waves(1)
            std(4)
            hi_tile(4, 0)

            def part1(m, s, more):
                t = NT * m + s
                std(t + 1)
                for part in ((0,), (1, 2), (3,), ())[s]:
                    taps_out(m, part)
                hi_tile(t + 1, s + 1)
                if s == 1 and more:
                    waves(m + 1)

            with act.Fori(1, HBLK - 1) as m:
                for s in range(NT):
                    part1(m, s, True)
            for s in range(NT):
                part1(HBLK - 1, s, False)

            t0 = NT * HBLK
            std(t0 + 1)
            hi_tile(t0 + 1, 1)
            for k in range(KC):
                act.wait_ge(a_ps, k + 1)
                nc.scalar.activation(a_hi[:, k, :, 0:2 * RANK],
                                     side[k % 2][:, 0:NB * RANK].rearrange("p (s r) -> p s r", s=NT), ACT.Copy)
                nc.scalar.activation(a_hi[:, k, :, 2 * RANK:LR],
                                     side[k % 2][:, NB * RANK:(NB + 1) * RANK].unsqueeze(1)
                                     .to_broadcast([P, NT, RANK]), ACT.Copy).then_inc(a_hi_ok, 1)
            for b in range(2):
                act.wait_ge(bt_ps, b + 1)
                for s in range(NT):
                    ins = nc.scalar.activation(
                        b_full[2 * RANK:LR, s, :].rearrange("q (o c) -> q c o", c=OPB)[:, 4 * b:4 * b + 4, :],
                        side[b][0:RANK, :].rearrange("q (c o) -> q c o", c=4), ACT.Copy)
                ins.then_inc(bt_ev, 1)
            for g in range(NG):
                if g == 0:
                    std(t0 + 2)
                if g == 2:
                    hi_tile(t0 + 2, 2)
                for b in range(2):
                    act.wait_ge(bt_ps, 2 * g + b + 3)
                    nc.scalar.activation(b_tr[:, g, :].rearrange("q (o c) -> q c o", c=OPB)[:, 4 * b:4 * b + 4, :],
                                         side[b][:, :].rearrange("q (c o) -> q c o", c=4), ACT.Copy)\
                      .then_inc(bt_ev, 1)
            std(t0 + 3)
            for j in range(4):
                half, quad = j // 2, j % 2
                act.wait_ge(bm_ps, j + 1)
                for o in range(2):
                    ins = nc.scalar.activation(b_full[0:2 * RANK, 2 * quad + o, half * HALF:(half + 1) * HALF],
                                               side[j % 2][64 * o:64 * o + 64, :], ACT.Copy)
                ins.then_inc(bm_ev, 1)
            hi_tile(t0 + 3, 3)
            std(G1)
            act.wait_ge(w2_in, 16)
            for k in range(KC):
                if k == KC // 2:
                    hi_tile(G1, 0)
                nc.scalar.activation(w2_hi[:, k, :], w2_raw[:, k, :], ACT.Copy).then_inc(w2_hi_ok, 1)
            std(G1 + 1)
            act.wait_ge(gemm_ok, G1)
            for s in range(NT):
                nc.scalar.activation(b_hi[:, s, :], b_full[:, s, :], ACT.Copy).then_inc(b_hi_ok, 1)

            def part2(g, s, more):
                t = G1 + NT * g + s
                act.wait_ge(ax_f_ok, t - G1 + 1)
                nc.scalar.activation(ax_hi[s % 2][0:LR, :], ax_f[:, :], ACT.Copy).then_inc(ax_hi_ok, 1)
                if more:
                    if not (isinstance(t, int) and t == G1):
                        std(t + 1)
                    hi_tile(t + 1, s + 1)

            for s in range(NT):
                part2(0, s, True)
            with act.Fori(1, HBLK) as g:
                for s in range(NT):
                    part2(g, s, True)
            for s in range(NT):
                part2(HBLK, s, s < NT - 1)

        @block.vector
        def _(dve):
            V = nc.vector
            count = {"n": 0, "base": 0}

            def then(ins):
                count["n"] += 1
                ins.then_inc(own, 1)
                dve.wait_ge(own, count["base"] + count["n"])

            def repeat(begin, end, per_iteration, body):
                first, start = count["n"], count["base"]
                with dve.Fori(begin, end) as i:
                    count["base"] = i * per_iteration + (start - begin * per_iteration)
                    body(i)
                assert count["n"] - first == per_iteration, count["n"] - first
                count["base"], count["n"] = start, first + (end - begin) * per_iteration

            def fused(dst, a, scalar, b, op0, op1, w):
                then(V.scalar_tensor_tensor(dst, a, scalar, b, op0, op1))

            W = lambda j: par[:, j, :]
            dve.wait_ge(par_in, 64)
            exp_parts(V, then, fused, W(1), XW, W(5), W(6), W(7), pint[:, :])
            V.scalar_tensor_tensor(W(8), W(7), 1.0, pint[:, :].bitcast(F32), ALU.add, ALU.mult).then_inc(exp_ok, 1)
            dve.wait_ge(const_ok, 1)
            V.tensor_copy(etab[:, :, :], etab_i[:, :, :]).then_inc(etab_ok, 1)
            dve.wait_ge(etab_ok, 1)

            def mask_sums(i):
                dve.wait_ge(w_in[i % 4], 32 * (i // 4 + 1))
                V.tensor_reduce(msum[i % 2][:, :], m_nat[i % 4][:, :].rearrange("p (k j) -> p k j", j=32),
                                AX.X, ALU.add).then_inc(msum_ok, 1)

            def mask_weight(i):
                dve.wait_ge(bs_ok, i + 1)
                rows = w_nat[i % 4][:, :].rearrange("p (k j) -> p k j", j=32)
                V.scalar_tensor_tensor(rows, acc[i % 2][:, HALF:HALF + D // 32].unsqueeze(2)
                                       .to_broadcast([P, D // 32, 32]), 0.0, rows,
                                       ALU.is_gt, ALU.mult).then_inc(mask_ok, 1)

            def lo_unit(u, hi, lo):
                for b in range(2):
                    dve.wait_ge(hi_ok, 2 * u + b + 1)
                    V.tensor_tensor(lo[:, 4 * b:4 * b + 4, :], tp[b][:, :].rearrange("p (k r) -> p k r", k=4),
                                    hi[:, 4 * b:4 * b + 4, :].bitcast(F32), ALU.subtract).then_inc(lo_ok, 1)

            def lo_weight(i):
                cols = slice(i * P, (i + 1) * P)
                lo_unit(weight_unit(i), w1_hi[:, :, cols], w1_lo[:, :, cols])

            def lo_tile(t, s):
                lo_unit(tile_unit(t), d_hi[s % 2], d_lo[s % 2])

            def variance(t, slot, in_count):
                dve.wait_ge(h_in[slot], in_count)
                V.bn_stats(stat[:, 0, :], h_t[slot][:, 0:HALF])
                V.bn_stats(stat[:, 1, :], h_t[slot][:, HALF:D])
                dve.drain()
                then(V.bn_aggr(mv[:, :], stat[:, :, :].rearrange("p a b -> p (a b)")))
                V.tensor_scalar(sc[:, 0:1], mv[:, 1:2], EPS, None, ALU.add).then_inc(var_ok, 1)

            def scale(t, slot):
                dve.wait_ge(sd_ok, t + 1)
                then(V.reciprocal(sc[:, 2:3], sc[:, 1:2]))
                then(V.scalar_tensor_tensor(sc[:, 3:4], sc[:, 2:3], sc[:, 2:3], sc[:, 0:1], ALU.mult, ALU.mult))
                then(V.tensor_scalar(sc[:, 3:4], sc[:, 3:4], -0.5, 1.5, ALU.mult, ALU.add))
                then(V.tensor_tensor(sc[:, 4:5], sc[:, 2:3], sc[:, 3:4], ALU.mult))
                if not (isinstance(t, int) and t == 0):
                    dve.wait_ge(tp_full, 2 * tile_unit(t - 1) + 2)
                V.tensor_scalar(d_t[:, :], h_t[slot][:, :], mv[:, 0:1], sc[:, 4:5], ALU.subtract, ALU.mult)\
                 .then_inc(d_ok, 1)

            def normalise(t, slot, in_count):
                variance(t, slot, in_count)
                scale(t, slot)

            def add_rows(t, s):
                dve.wait_ge(gemm_ok, t + 1)
                V.tensor_tensor(h_t[s][:, :], acc[s % 2][:, :], h_t[s][:, :], ALU.add).then_inc(acc_free, 1)

            def nearest():
                return V.tensor_scalar(mag[:, :, :], turn[:, :, :], MAGIC, MAGIC, ALU.add, ALU.subtract)

            def magnitudes():
                V.tensor_scalar(mag[:, :, :].bitcast(I32), turn[:, :, :].bitcast(I32), 0x7FFFFFFF, None,
                                ALU.bitwise_and).then_inc(tab_ok, 1)

            def turns(m):
                then(raw_turns(V, m))
                then(nearest())
                then(V.tensor_tensor(turn[:, :, :], turn[:, :, :], mag[:, :, :], ALU.subtract))
                exponents(V, m)
                magnitudes()

            def tables(m):
                dve.wait_ge(wave_ok, m + 1)
                w0, e0 = 0, 0
                for n in (NB0, NB1):
                    pair = wave[:, :, w0:w0 + 2 * n].rearrange("p h (z n) -> p h z n", z=2)
                    V.tensor_tensor(pair, pair, decay[:, :, e0:e0 + n].unsqueeze(2).to_broadcast([P, GR, 2, n]),
                                    ALU.mult)
                    w0, e0 = w0 + 2 * n, e0 + n
                then(V.tensor_tensor(fdec[:, :, :, :],
                                     modes[:, 4:6, bass.ds(GR * m, GR)].unsqueeze(3).to_broadcast([P, 2, GR, NA]),
                                     decay[:, :, e0:e0 + NA].unsqueeze(1).to_broadcast([P, 2, GR, NA]), ALU.mult))
                if not (isinstance(m, int) and m == 0):
                    dve.wait_ge(l_ok, NT * m)
                for z, dst in ((0, lead), (1, lead2)):
                    ins = V.tensor_tensor(dst[:, :, :, :],
                                          wave[:, :, w0 + z * NA:w0 + (z + 2) * NA]
                                          .rearrange("p h (z n) -> p z h n", z=2),
                                          fdec[:, z, :, :].unsqueeze(1).to_broadcast([P, 2, GR, NA]), ALU.mult)
                then(ins)
                V.tensor_tensor(lead[:, :, :, :], lead[:, :, :, :], lead2[:, :, :, :], ALU.add).then_inc(lead_ok, 1)
                dve.wait_ge(lead_ok, m + 1)

            def factors(m, s):
                q = NT * m + s
                hs = slice(HS * s, HS * (s + 1))
                first = isinstance(m, int) and q == 0
                if not (isinstance(m, int) and q < 2):
                    dve.wait_ge(k_ok, KU + 2 * q - 2)
                w1 = 2 * NB0
                r4 = right[s % 2][:, :, :].rearrange("p h (b a) -> p h b a", a=NB0)
                t4 = rtmp[:, :, :].rearrange("p h (b a) -> p h b a", a=NB0)

                def outer(dst, w, x0):
                    return V.tensor_tensor(dst, wave[:, hs, w:w + NB1].unsqueeze(3).to_broadcast([P, HS, NB1, NB0]),
                                           wave[:, hs, x0:x0 + NB0].unsqueeze(2).to_broadcast([P, HS, NB1, NB0]),
                                           ALU.mult)

                outer(r4, w1, 0)
                if not first:
                    dve.wait_ge(r_ok, q)
                outer(t4, w1 + NB1, NB0).then_inc(rmul_ok, 1)
                V.tensor_tensor(left[s % 2][:, :, :, :],
                                c_re[:, bass.ds(GR * m + HS * s, HS), :].unsqueeze(3).to_broadcast([P, HS, CH, NA]),
                                lead[:, 0, hs, :].unsqueeze(2).to_broadcast([P, HS, CH, NA]), ALU.mult)\
                 .then_inc(lmul_ok, 1)
                if isinstance(m, int) and m == 0:
                    dve.wait_ge(lmul_ok, q + 1)
                    dve.wait_ge(ltmp_ok, q + 1)
                    V.tensor_tensor(left[s % 2][:, :, :, :], left[s % 2][:, :, :, :], ltmp[:, :, :, :], ALU.add)\
                     .then_inc(l_ok, 1)

            def text(t):
                normalise(t, t, h_count(1, 0))

            mask_sums(0)
            mask_weight(0)
            mask_sums(1)
            mask_weight(1)
            lo_weight(0)
            text(0)
            mask_sums(2)
            lo_weight(1)
            mask_sums(3)
            mask_weight(2)
            lo_tile(0, 0)
            mask_weight(3)
            lo_weight(2)
            dve.wait_ge(den_ok, 1)
            V.reciprocal(par[:, 14, 0:N], par[:, 14, 0:N]).then_inc(recip_ok, 1)
            lo_weight(3)
            mask_sums(4)
            mask_sums(5)
            text(1)
            lo_tile(1, 1)
            mask_weight(4)
            mask_sums(6)
            mask_weight(5)
            lo_weight(4)
            mask_sums(7)
            mask_weight(6)
            lo_weight(5)
            mask_weight(7)
            variance(2, 2, h_count(1, 0))
            dve.wait_ge(turn0_ok, 1)
            nearest().then_inc(whole0_ok, 1)
            scale(2, 2)
            lo_weight(6)
            dve.wait_ge(turn0_ok, 3)
            magnitudes()
            lo_weight(7)
            variance(3, 3, h_count(1, 0))
            add_rows(0, 0)
            tables(0)
            lo_tile(2, 2)
            scale(3, 3)
            factors(0, 0)
            factors(0, 1)
            add_rows(1, 1)
            lo_tile(3, 3)
            factors(0, 2)
            factors(0, 3)
            turns(1)
            add_rows(2, 2)
            tables(1)
            normalise(4, 0, h_count(1, 1))
            factors(1, 0)
            lo_tile(4, 0)
            factors(1, 1)
            add_rows(3, 3)

            def part1(m, s, more):
                t = NT * m + s
                normalise(t + 1, (s + 1) % NT, h_count(1, m + (s + 1) // NT))
                if s == 0 and more:
                    turns(m + 1)
                elif s == 1:
                    factors(m, 3)
                elif s == 2 and more:
                    tables(m + 1)
                lo_tile(t + 1, s + 1)
                if s == 0:
                    factors(m, 2)
                elif s >= 2 and more:
                    factors(m + 1, s - 2)
                add_rows(t, s)

            OWN_PART1 = 25
            repeat(1, HBLK - 1, OWN_PART1, lambda m: [part1(m, s, True) for s in range(NT)])
            for s in range(NT):
                part1(HBLK - 1, s, False)

            t0 = NT * HBLK
            then(V.tensor_reduce(rank_id[:, :], ident[:, :].rearrange("p (j r) -> p r j", r=RANK), AX.X, ALU.add))
            dve.wait_ge(col_ok, 1)
            then(V.tensor_copy(g_col[:, :, :], side[0][:, 0:NG * NB].rearrange("p (g b) -> p g b", g=NG)))
            V.tensor_tensor(g_mat[:, :, :].rearrange("p g (b r) -> p (g b) r", r=RANK),
                            g_col[:, :, :].rearrange("p g b -> p (g b)").unsqueeze(2)
                            .to_broadcast([P, NG * NB, RANK]),
                            rank_id[:, :].unsqueeze(1).to_broadcast([P, NG * NB, RANK]), ALU.mult)\
             .then_inc(g_ok, 1)
            normalise(t0 + 1, 1, h_count(1, HBLK))
            lo_tile(t0 + 1, 1)
            add_rows(t0, 0)
            for k in range(KC):
                dve.wait_ge(a_hi_ok, k + 1)
                V.tensor_tensor(a_lo[:, k, :, 0:2 * RANK],
                                side[k % 2][:, 0:NB * RANK].rearrange("p (s r) -> p s r", s=NT),
                                a_hi[:, k, :, 0:2 * RANK].bitcast(F32), ALU.subtract)
                V.tensor_tensor(a_lo[:, k, :, 2 * RANK:LR],
                                side[k % 2][:, NB * RANK:(NB + 1) * RANK].unsqueeze(1).to_broadcast([P, NT, RANK]),
                                a_hi[:, k, :, 2 * RANK:LR].bitcast(F32), ALU.subtract).then_inc(a_lo_ok, 1)
            normalise(t0 + 2, 2, h_count(1, HBLK))
            lo_tile(t0 + 2, 2)
            add_rows(t0 + 1, 1)
            normalise(t0 + 3, 3, h_count(1, HBLK))
            lo_tile(t0 + 3, 3)
            add_rows(t0 + 2, 2)
            normalise(G1, 0, h_count(2, 0))

            def w2_low(k):
                dve.wait_ge(w2_hi_ok, k + 1)
                V.tensor_tensor(w2_lo[:, k, :], w2_raw[:, k, :], w2_hi[:, k, :].bitcast(F32), ALU.subtract)\
                 .then_inc(w2_lo_ok, 1)

            for k in range(KC // 2):
                w2_low(k)
            lo_tile(G1, 0)
            normalise(G1 + 1, 1, h_count(2, 0))
            for k in range(KC // 2, KC):
                w2_low(k)
            add_rows(t0 + 3, 3)

            def split_up(s):
                dve.wait_ge(b_hi_ok, s + 1)
                V.tensor_tensor(b_lo[:, s, :], b_full[:, s, :], b_hi[:, s, :].bitcast(F32), ALU.subtract)\
                 .then_inc(b_lo_ok, 1)

            dve.wait_ge(rows_ok, 1)

            def part2(g, s, more):
                t = G1 + NT * g + s
                dve.wait_ge(ax_ps, t - G1 + 1)
                then(V.tensor_tensor(ax_f[:, :], side[s % 2][0:LR, 0:P], own_rows[:, :], ALU.mult))
                then(V.tensor_tensor(ax_g[:, :], side[s % 2][0:LR, P:2 * P], own_rows[:, :], ALU.mult))
                V.tensor_tensor(ax_f[:, :], ax_f[:, :], ax_g[:, :], ALU.add).then_inc(ax_f_ok, 1)
                dve.wait_ge(ax_hi_ok, t - G1 + 1)
                V.tensor_tensor(ax_lo[s % 2][0:LR, :], ax_f[:, :], ax_hi[s % 2][0:LR, :].bitcast(F32), ALU.subtract)\
                 .then_inc(ax_lo_ok, 1)
                if isinstance(t, int) and t < G1 + NT:
                    split_up(s)
                if more:
                    if not (isinstance(t, int) and t == G1):
                        normalise(t + 1, (s + 1) % NT, h_count(2, g + (s + 1) // NT))
                    lo_tile(t + 1, s + 1)
                add_rows(t, s)

            OWN_PART2 = 28
            for s in range(NT):
                part2(0, s, True)
            repeat(1, HBLK, OWN_PART2, lambda g: [part2(g, s, True) for s in range(NT)])
            for s in range(NT):
                part2(HBLK, s, s < NT - 1)

        @block.tensor
        def _(pe):
            mm = nc.tensor.matmul
            pe.wait_ge(const_ok, 1)

            def c_transposes(g):
                pe.wait_ge(dup_ok, g + 1)
                fill = g if g < 2 else g + 2
                if fill >= 2:
                    pe.wait_ge(k_ev, fill - 1)
                for j in range(4):
                    c, z = 4 * (g % 4) + j, g // 4
                    ins = nc.tensor.transpose(side[g % 2][:, j * P:(j + 1) * P],
                                              x_dup[:, z, c, :, :].rearrange("h t n -> h (t n)"), ident[:, :])
                ins.then_inc(k_ok, 1)

            def mode_transposes():
                pe.wait_ge(k_ev, 2)
                pe.wait_ge(modes_ok, 1)
                for g, n in ((0, 4), (1, 2)):
                    for j in range(n):
                        ins = nc.tensor.transpose(side[g][:, j * P:(j + 1) * P],
                                                  modes_in[:, 4 * g + j, :, :].rearrange("h z n -> h (z n)"), ident[:, :])
                    ins.then_inc(k_ok, 1)

            def block_sums(i):
                pe.wait_ge(msum_ok, i + 1)
                if i >= 2:
                    pe.wait_ge(mask_ok, i - 1)
                mm(acc[i % 2][:, HALF:HALF + D // 32], blocks[:, :], msum[i % 2][:, :], start=True, stop=True)\
                  .then_inc(bs_ok, 1)

            def transposes(u, src, first=False):
                for b in range(2):
                    if not first:
                        pe.wait_ge(lo_ok, 2 * u - 1 + b)
                    for j in range(4):
                        k = 4 * b + j
                        ins = nc.tensor.transpose(tp[b][:, j * P:(j + 1) * P], src[:, k * P:(k + 1) * P], ident[:, :])
                    ins.then_inc(tp_full, 1)

            def weight_tile(i):
                pe.wait_ge(mask_ok, i + 1)
                transposes(weight_unit(i), w_nat[i % 4], i == 0)

            def split_mm(dst, l_hi, l_lo, r_hi, r_lo, start, stop):
                mm(dst, l_hi, r_hi, start=start, stop=False)
                mm(dst, l_hi, r_lo, start=False, stop=False)
                return mm(dst, l_lo, r_hi, start=False, stop=stop)

            def tile_transposes(t):
                pe.wait_ge(d_ok, t + 1)
                transposes(tile_unit(t), d_t)

            def product(s, chunks, r_hi, r_lo, end, halves=(0, 1)):
                for k in chunks:
                    for half in halves:
                        cols = slice(half * HALF, (half + 1) * HALF)
                        ins = split_mm(acc[s % 2][:, cols], d_hi[s % 2][:, k, :], d_lo[s % 2][:, k, :],
                                       r_hi[:, k, cols], r_lo[:, k, cols], k == 0, end and k == KC - 1)
                return ins

            def begin(t):
                pe.wait_ge(lo_ok, 2 * tile_unit(t) + 2)
                if not (isinstance(t, int) and t < 2):
                    pe.wait_ge(acc_free, t - 1)

            FIRST, SECOND = range(0, KC // 2), range(KC // 2, KC)

            def tile1(t, s, taps=None, early_taps=None, split=KC // 2):
                begin(t)
                if early_taps is not None:
                    tap_products(*early_taps)
                product(s, range(0, split), w1_hi, w1_lo, True)
                if taps is not None:
                    tap_products(*taps)
                tile_transposes(t + 1)
                product(s, range(split, KC), w1_hi, w1_lo, True).then_inc(gemm_ok, 1)

            def tap_products(m, s):
                q = NT * m + s
                pe.wait_ge(r_ok, q + 1)
                pe.wait_ge(l_ok, q + 1)
                pe.wait_ge(k_ev, KU + 2 * q)
                for h in range(HS):
                    ins = mm(side[h // 4][:, (h % 4) * STEP:(h % 4 + 1) * STEP],
                             left[s % 2][:, h, :, :].rearrange("p c a -> p (c a)"), right[s % 2][:, h, :],
                             start=True, stop=True)
                    if h % 4 == 3:
                        ins.then_inc(k_ok, 1)

            block_sums(0)
            block_sums(1)
            weight_tile(0)
            weight_tile(1)
            block_sums(2)
            tile_transposes(0)
            block_sums(3)
            weight_tile(2)
            weight_tile(3)
            pe.wait_ge(lo_ok, 2 * weight_unit(3) + 2)
            product(0, FIRST, w1_hi, w1_lo, True, (0,))
            block_sums(4)
            block_sums(5)
            tile_transposes(1)
            c_transposes(0)
            c_transposes(1)
            product(0, SECOND, w1_hi, w1_lo, True, (0,))
            begin(1)
            for i, chunks in ((4, FIRST), (5, SECOND), (6, None), (7, None)):
                weight_tile(i)
                if i < 6:
                    block_sums(i + 2)
                    if i == 4:
                        mode_transposes()
                    product(1, chunks, w1_hi, w1_lo, True, (0,))
                if i < 7:
                    c_transposes(2 * i - 6)
                    c_transposes(2 * i - 5)
            tile_transposes(2)
            for k in (FIRST, SECOND):
                ins = product(0, k, w1_hi, w1_lo, True, (1,))
            ins.then_inc(gemm_ok, 1)
            product(1, range(0, KC), w1_hi, w1_lo, True, (1,)).then_inc(gemm_ok, 1)
            begin(2)
            product(2, range(0, 5), w1_hi, w1_lo, True)
            tap_products(0, 0)
            tile_transposes(3)
            product(2, range(5, KC), w1_hi, w1_lo, True).then_inc(gemm_ok, 1)
            tap_products(0, 1)
            begin(3)
            product(3, range(0, 3), w1_hi, w1_lo, True)
            tap_products(0, 2)
            product(3, range(3, 6), w1_hi, w1_lo, True)
            tap_products(0, 3)
            product(3, range(6, KC), w1_hi, w1_lo, True).then_inc(gemm_ok, 1)
            tile_transposes(4)

            def block1(m):
                for s in range(NT):
                    tile1(NT * m + s, s, {0: (m, 0), 1: (m, 2)}.get(s), {1: (m, 1), 2: (m, 3)}.get(s),
                          KC // 2 + (1 if s == 3 else 0))

            with pe.Fori(1, HBLK) as m:
                block1(m)

            t0 = NT * HBLK
            pe.wait_ge(sel_ok, 1)
            pe.wait_ge(k_ev, KU + 2 * t0)
            for g in range(NG):
                ins = mm(side[0][:, g * NB:(g + 1) * NB], g_sel[:, g, :], gate_t[:, :], start=True, stop=True)
            ins.then_inc(col_ok, 1)
            tile1(t0, 0)
            pe.wait_ge(g_ok, 1)
            pe.wait_ge(la_in, 32)
            for k in range(KC):
                if k >= 2:
                    pe.wait_ge(a_lo_ok, k - 1)
                cols = slice(k * P, (k + 1) * P)
                for g in range(NG):
                    mm(side[k % 2][:, 0:NB * RANK], a_nat[:, g, cols], g_mat[:, g, :], start=(g == 0), stop=(g == NG - 1))
                nc.tensor.transpose(side[k % 2][:, NB * RANK:(NB + 1) * RANK], as_nat[:, cols], ident[0:RANK, 0:RANK])\
                  .then_inc(a_ps, 1)
            pe.wait_ge(a_lo_ok, KC)
            pe.wait_ge(lb_in, 48)
            def up_transposes(g):
                if g < NG:
                    pe.wait_ge(bl_ok, g + 1)
                for b in range(2):
                    n = 2 * ((g + 1) % (NG + 1)) + b
                    if n >= 2:
                        pe.wait_ge(bt_ev, n - 1)
                    for j in range(4):
                        c = 4 * b + j
                        if g < NG:
                            ins = nc.tensor.transpose(side[b][:, j * P:(j + 1) * P],
                                                      bl_by_o[:, g, c, :, :].rearrange("p n r -> p (n r)"), ident[:, :])
                        else:
                            ins = nc.tensor.transpose(side[b][0:RANK, j * P:(j + 1) * P], bs_nat[:, c, :], ident[:, :])
                    ins.then_inc(bt_ps, 1)

            up_transposes(NG)
            begin(t0 + 1)
            for g in range(NG):
                ins = product(1, range(2 * g, 2 * g + 2), w1_hi, w1_lo, True)
                if g == NG - 1:
                    ins.then_inc(gemm_ok, 1)
                up_transposes(g)
                if g == 1:
                    tile_transposes(t0 + 2)
            pe.wait_ge(bt_ev, 2 * NG + 2)
            for j in range(4):
                half, quad = j // 2, j % 2
                if j >= 2:
                    pe.wait_ge(bm_ev, j - 1)
                for g in range(NG):
                    ins = mm(side[j % 2][:, :], g_mat[:, g, quad * P:(quad + 1) * P],
                             b_tr[:, g, half * HALF:(half + 1) * HALF], start=(g == 0), stop=(g == NG - 1))
                ins.then_inc(bm_ps, 1)
            for s in range(2, NT):
                tile1(t0 + s, s)

            pe.wait_ge(bm_ev, 4)

            def down(t, s):
                for k in range(KC):
                    both = d_hl[s % 2][:, k, :, :].rearrange("p z r -> p (z r)")
                    mm(side[s % 2][0:LR, 0:2 * P], a_hi[:, k, s, :], both, start=(k == 0), stop=False)
                    ins = mm(side[s % 2][0:LR, 0:2 * P], a_lo[:, k, s, :], both, start=False, stop=(k == KC - 1))
                ins.then_inc(ax_ps, 1)

            MIDDLE = 5

            def up(t, s):
                pe.wait_ge(ax_lo_ok, t - G1 + 1)
                for half in range(2):
                    cols = slice(half * HALF, (half + 1) * HALF)
                    ins = split_mm(acc[s % 2][:, cols], ax_hi[s % 2][:, :], ax_lo[s % 2][:, :],
                                   b_hi[:, s, cols], b_lo[:, s, cols], False, True)
                return ins

            def tile2(g, s, more, first=False):
                t = G1 + NT * g + s
                begin(t)
                down(t, s)
                for k in range(0, MIDDLE):
                    if first:
                        pe.wait_ge(w2_lo_ok, k + 1)
                    product(s, [k], w2_hi, w2_lo, False)
                if more:
                    tile_transposes(t + 1)
                for k in range(MIDDLE, KC):
                    if first:
                        pe.wait_ge(w2_lo_ok, k + 1)
                    product(s, [k], w2_hi, w2_lo, False)
                if isinstance(g, int) and g == 0:
                    pe.wait_ge(b_lo_ok, s + 1)
                up(t, s).then_inc(gemm_ok, 1)

            for s in range(NT):
                tile2(0, s, True, first=s == 0)
            with pe.Fori(1, HBLK) as g:
                for s in range(NT):
                    tile2(g, s, True)
            for s in range(NT):
                tile2(HBLK, s, s < NT - 1)


_INS = ['x', 'txt', 'L0_tok_log_dt', 'L0_tok_B', 'L0_tok_inv_A_real', 'L0_tok_A_imag', 'L0_attn_weight',
        'L0_attn_mask', 'L0_ffn_gate', 'L0_ffn_kernel', 'L0_ffn_bias', 'L0_ffn_lora_A', 'L0_ffn_lora_B',
        'L0_ffn_lora_A_shared', 'L0_ffn_lora_B_shared']
_OUTS = [((16, 160, 1024), 'float32')]


def kernel(**inputs):
    import numpy as _np
    import concourse.bacc as _bacc
    from concourse import mybir as _mybir
    from concourse.bass_utils import run_bass_kernel_spmd as _run

    nc = _bacc.Bacc("TRN2", target_bir_lowering=False, num_devices=1)
    arrays, args = {}, []
    for name in _INS:
        a = _np.ascontiguousarray(inputs[name])
        arrays[f"in_{name}_dram"] = a
        args.append(nc.dram_tensor(f"in_{name}_dram", a.shape, _mybir.dt.from_np(a.dtype), kind="ExternalInput").ap())
    for i, (shape, dtype) in enumerate(_OUTS):
        dt = _mybir.dt.from_np(_np.dtype(dtype))
        args.append(nc.dram_tensor(f"out_{i}_dram", shape, dt, kind="ExternalOutput").ap())
    build_fusion_layer(nc, *args)
    r = _run(nc, [arrays], core_ids=[0])
    got = tuple(r.results[0][f"out_{i}_dram"] for i in range(len(_OUTS)))
    return got[0]
```
